# Optimizing a Trainium2 kernel written in Bass

```python
import numpy as np
import jax
import jax.numpy as jnp

def _softmax(x, axis=-1):
    return jax.nn.softmax(x, axis=axis)

def _gelu(x):
    return jax.nn.gelu(x, approximate=True)

def _silu(x):
    return jax.nn.silu(x)

def _sigmoid(x):
    return jax.nn.sigmoid(x)

def _layernorm(x, axis=-1, eps=1e-05):
    m = jnp.mean(x, axis=axis, keepdims=True)
    v = jnp.var(x, axis=axis, keepdims=True)
    return (x - m) / jnp.sqrt(v + eps)

def _scatter_add(tgt, idx, src, axis=0):
    return tgt.at[idx].add(src)

def _segment_sum(src, seg, n):
    return jax.ops.segment_sum(src, seg, n)
kernel_name = 'mk_recurrent_d2_jaxref_r4_f470d2'

def setup_inputs(seed: int=0):
    np.random.seed(seed)
    _w = jnp.asarray

    def _L0_attn_setup():
        import jax, jax.numpy as jnp
        import numpy as np
        GAMMA = 0.96875
        H = 256
        B = 4
        L = 512
        key = jax.random.key(seed)
        k0, k1, k2, k3, k4 = jax.random.split(key, 5)
        x = jax.random.normal(k0, (B, L, H), dtype=jnp.float32)
        weight_q = jax.random.normal(k1, (H, H), dtype=jnp.float32) / H
        weight_k = jax.random.normal(k2, (H, H), dtype=jnp.float32) / H
        weight_v = jax.random.normal(k3, (H, H), dtype=jnp.float32) / H
        theta = jax.random.normal(k4, (H,), dtype=jnp.float32) / H
        return {'x': x, 'weight_q': weight_q, 'weight_k': weight_k, 'weight_v': weight_v, 'theta': theta}
    _L0_attn_in = _L0_attn_setup()

    def _L0_ffn_setup():
        import jax, jax.numpy as jnp
        import numpy as np
        B, L, H = (8, 512, 256)
        E, K, R = (8, 2, 64)

        def _gates(cls_tok, Wr):
            logits = cls_tok @ Wr.T
            top_vals, top_idx = jax.lax.top_k(logits, K)
            neg_inf = jnp.full_like(logits, -jnp.inf)
            rows = jnp.arange(logits.shape[0])[:, None]
            masked = neg_inf.at[rows, top_idx].set(top_vals)
            return jax.nn.softmax(masked, axis=-1)
        key = jax.random.key(seed)
        k1, k2, k3, k4 = jax.random.split(key, 4)
        x = jax.random.normal(k1, (B, L, H), dtype=jnp.float32)
        Wr = jax.random.normal(k2, (E, H), dtype=jnp.float32) * (1.0 / np.sqrt(H))
        A = jax.random.normal(k3, (E, R, H), dtype=jnp.float32) * (1.0 / np.sqrt(H))
        Bw = jax.random.normal(k4, (E, H, R), dtype=jnp.float32) * (1.0 / np.sqrt(R))
        return {'x': x, 'Wr': Wr, 'A': A, 'Bw': Bw}
    _L0_ffn_in = _L0_ffn_setup()

    def _L1_attn_setup():
        import jax, jax.numpy as jnp
        import numpy as np
        import math
        BATCH, SEQLEN, DMODEL, NSTATE, DFF = (4, 512, 256, 16, 1024)
        EPS = 1e-06

        def rmsnorm(x, scale):
            return x * jax.lax.rsqrt(jnp.mean(x * x, axis=-1, keepdims=True) + EPS) * scale

        def ssm_scan(u, A_ssm, B_ssm, C_ssm, D_ssm):
            dt = jnp.exp(jnp.linspace(math.log(0.001), math.log(0.1), NSTATE))
            expA = jnp.exp(A_ssm)
            dA = jnp.exp(-expA * dt)
            dB = B_ssm * (1.0 - dA) / expA

            def step(s, u_t):
                s = s * dA + u_t[..., None] * dB
                y = jnp.einsum('bdn,dn->bd', s, C_ssm)
                return (s, y)
            s0 = jnp.zeros((u.shape[0], DMODEL, NSTATE), dtype=u.dtype)
            _, ys = jax.lax.scan(step, s0, jnp.transpose(u, (1, 0, 2)))
            return jnp.transpose(ys, (1, 0, 2)) + u * D_ssm
        key = jax.random.key(seed)
        ks = jax.random.split(key, 6)
        return {'x': jax.random.normal(ks[0], (BATCH, SEQLEN, DMODEL), jnp.float32), 'A_ssm': jax.random.normal(ks[1], (DMODEL, NSTATE), jnp.float32), 'B_ssm': jax.random.normal(ks[2], (DMODEL, NSTATE), jnp.float32), 'C_ssm': jax.random.normal(ks[3], (DMODEL, NSTATE), jnp.float32), 'D_ssm': jnp.zeros((DMODEL,), jnp.float32), 'scale1': jnp.ones((DMODEL,), jnp.float32), 'scale2': jnp.ones((DMODEL,), jnp.float32), 'w1': jax.random.normal(ks[4], (DMODEL, DFF), jnp.float32) * 0.02, 'b1': jnp.zeros((DFF,), jnp.float32), 'w2': jax.random.normal(ks[5], (DFF, DMODEL), jnp.float32) * 0.02, 'b2': jnp.zeros((DMODEL,), jnp.float32)}
    _L1_attn_in = _L1_attn_setup()

    def _L1_ffn_setup():
        import jax, jax.numpy as jnp
        import numpy as np
        import math
        B, T, D, H, E, TOPK, CAPF = (4, 512, 256, 16, 8, 2, 2.0)
        HD = D // H

        def layernorm(x, g, b, eps=1e-05):
            m = jnp.mean(x, -1, keepdims=True)
            v = jnp.mean(jnp.square(x - m), -1, keepdims=True)
            return (x - m) * jax.lax.rsqrt(v + eps) * g + b

        def block_forward(x, ln1_g, ln1_b, Wqkv, Wproj, ln2_g, ln2_b, Wgate, W1, b1, W2, b2):
            Bb, Tt, d = x.shape
            hd = HD
            half = hd // 2
            h = layernorm(x, ln1_g, ln1_b)
            qkv = (h @ Wqkv).reshape(Bb, Tt, H, 3 * hd)
            q, k, v = (qkv[..., :hd], qkv[..., hd:2 * hd], qkv[..., 2 * hd:])
            inv_freq = 1.0 / 10000.0 ** (jnp.arange(0, hd, 2, dtype=jnp.float32) / hd)
            ang = jnp.arange(Tt, dtype=jnp.float32)[:, None] * inv_freq
            sin = jnp.sin(ang)[None, :, None, :].astype(x.dtype)
            cos = jnp.cos(ang)[None, :, None, :].astype(x.dtype)

            def rope(t):
                t1, t2 = (t[..., :half], t[..., half:])
                return jnp.concatenate([t1 * cos - t2 * sin, t1 * sin + t2 * cos], -1)
            q, k = (rope(q), rope(k))
            scores = jnp.einsum('bqhd,bkhd->bhqk', q, k) / math.sqrt(hd)
            causal = jnp.tril(jnp.ones((Tt, Tt), dtype=bool))
            scores = jnp.where(causal, scores, jnp.asarray(-1000000000.0, scores.dtype))
            probs = jax.nn.softmax(scores, axis=-1)
            attn = jnp.einsum('bhqk,bkhd->bqhd', probs, v).reshape(Bb, Tt, d) @ Wproj
            x = x + attn
            h2 = layernorm(x, ln2_g, ln2_b)
            flat = h2.reshape(-1, d)
            N = flat.shape[0]
            capacity = int(math.ceil(CAPF * N / E))
            gates = jax.nn.softmax((flat @ Wgate).astype(jnp.float32), -1).astype(flat.dtype)
            _, top_inds = jax.lax.top_k(gates, TOPK)
            mask = jnp.zeros((N, E), dtype=bool).at[jnp.arange(N)[:, None], top_inds].set(True)
            pos = jnp.cumsum(mask.astype(jnp.int32), axis=0) * mask - 1
            keep = (pos < capacity) & mask
            t_flat = jnp.repeat(jnp.arange(N), TOPK)
            e_flat = top_inds.reshape(-1)
            p = pos[t_flat, e_flat]
            kp = keep[t_flat, e_flat]
            p_eff = jnp.where(kp, p, capacity)
            exp_in = jnp.zeros((E, capacity, d), flat.dtype).at[e_flat, p_eff].set(flat[t_flat], mode='drop')
            hmid = jax.nn.gelu(jnp.einsum('ecd,edf->ecf', exp_in, W1) + b1[:, None, :], approximate=False)
            exp_out = jnp.einsum('ecf,efd->ecd', hmid, W2) + b2[:, None, :]
            gate = gates[t_flat, e_flat] * kp.astype(flat.dtype)
            p_g = jnp.minimum(p_eff, capacity - 1)
            moe = jnp.zeros((N, d), flat.dtype).at[t_flat].add(exp_out[e_flat, p_g] * gate[:, None])
            return x + moe.reshape(Bb, Tt, d)
        key = jax.random.key(seed)
        ks = jax.random.split(key, 8)
        s = 0.02
        return {'x': jax.random.normal(ks[0], (B, T, D), jnp.float32), 'ln1_g': jnp.ones((D,), jnp.float32), 'ln1_b': jnp.zeros((D,), jnp.float32), 'Wqkv': jax.random.normal(ks[1], (D, 3 * D), jnp.float32) * s, 'Wproj': jax.random.normal(ks[2], (D, D), jnp.float32) * s, 'ln2_g': jnp.ones((D,), jnp.float32), 'ln2_b': jnp.zeros((D,), jnp.float32), 'Wgate': jax.random.normal(ks[3], (D, E), jnp.float32) * s, 'W1': jax.random.normal(ks[4], (E, D, 4 * D), jnp.float32) * s, 'b1': jnp.zeros((E, 4 * D), jnp.float32), 'W2': jax.random.normal(ks[5], (E, 4 * D, D), jnp.float32) * s, 'b2': jnp.zeros((E, D), jnp.float32)}
    _L1_ffn_in = _L1_ffn_setup()
    _d = {'L0_attn_x': _L0_attn_in['x'], 'L0_attn_weight_q': _L0_attn_in['weight_q'], 'L0_attn_weight_k': _L0_attn_in['weight_k'], 'L0_attn_weight_v': _L0_attn_in['weight_v'], 'L0_attn_theta': _L0_attn_in['theta'], 'L0_ffn_Wr': _L0_ffn_in['Wr'], 'L0_ffn_A': _L0_ffn_in['A'], 'L0_ffn_Bw': _L0_ffn_in['Bw'], 'L1_attn_A_ssm': _L1_attn_in['A_ssm'], 'L1_attn_B_ssm': _L1_attn_in['B_ssm'], 'L1_attn_C_ssm': _L1_attn_in['C_ssm'], 'L1_attn_D_ssm': _L1_attn_in['D_ssm'], 'L1_attn_scale1': _L1_attn_in['scale1'], 'L1_attn_scale2': _L1_attn_in['scale2'], 'L1_attn_w1': _L1_attn_in['w1'], 'L1_attn_b1': _L1_attn_in['b1'], 'L1_attn_w2': _L1_attn_in['w2'], 'L1_attn_b2': _L1_attn_in['b2'], 'L1_ffn_ln1_g': _L1_ffn_in['ln1_g'], 'L1_ffn_ln1_b': _L1_ffn_in['ln1_b'], 'L1_ffn_Wqkv': _L1_ffn_in['Wqkv'], 'L1_ffn_Wproj': _L1_ffn_in['Wproj'], 'L1_ffn_ln2_g': _L1_ffn_in['ln2_g'], 'L1_ffn_ln2_b': _L1_ffn_in['ln2_b'], 'L1_ffn_Wgate': _L1_ffn_in['Wgate'], 'L1_ffn_W1': _L1_ffn_in['W1'], 'L1_ffn_b1': _L1_ffn_in['b1'], 'L1_ffn_W2': _L1_ffn_in['W2'], 'L1_ffn_b2': _L1_ffn_in['b2']}
    _x0 = _d['L0_attn_x']
    _d['L0_attn_x'] = jax.random.normal(jax.random.fold_in(jax.random.key(seed), 1), (8, 1024, 256), dtype=_x0.dtype)
    del _x0
    return _d

def reference(L0_attn_x, L0_attn_weight_q, L0_attn_weight_k, L0_attn_weight_v, L0_attn_theta, L0_ffn_Wr, L0_ffn_A, L0_ffn_Bw, L1_attn_A_ssm, L1_attn_B_ssm, L1_attn_C_ssm, L1_attn_D_ssm, L1_attn_scale1, L1_attn_scale2, L1_attn_w1, L1_attn_b1, L1_attn_w2, L1_attn_b2, L1_ffn_ln1_g, L1_ffn_ln1_b, L1_ffn_Wqkv, L1_ffn_Wproj, L1_ffn_ln2_g, L1_ffn_ln2_b, L1_ffn_Wgate, L1_ffn_W1, L1_ffn_b1, L1_ffn_W2, L1_ffn_b2):

    def _L0_attn_ref(x, weight_q, weight_k, weight_v, theta):
        import jax, jax.numpy as jnp
        import numpy as np
        GAMMA = 0.96875
        H = 256
        B = 4
        L = 512
        Bb, Ll, Hh = x.shape
        dt = x.dtype
        seq = jnp.arange(1, Ll + 1, dtype=dt)
        zero = jnp.asarray(0.0, dtype=dt)
        thetas = jnp.exp(zero * seq[:, None] * theta[None, :])
        theta_conj = thetas
        q = jnp.matmul(x, weight_q) * thetas[None]
        k = jnp.matmul(x, weight_k) * theta_conj[None]
        v = jnp.matmul(x, weight_v)
        n = jnp.arange(Ll)
        diff = n[:, None] - n[None, :]
        D = jnp.where(diff >= 0, jnp.asarray(GAMMA, dt) ** diff.astype(dt), jnp.zeros((), dt))
        scores = jnp.einsum('bid,bjd->bij', q, k) * D[None]
        return jnp.einsum('bij,bjd->bid', scores, v)

    def _L0_ffn_ref(x, Wr, A, Bw):
        import jax, jax.numpy as jnp
        import numpy as np
        B, L, H = (8, 512, 256)
        E, K, R = (8, 2, 64)

        def _gates(cls_tok, Wr):
            logits = cls_tok @ Wr.T
            top_vals, top_idx = jax.lax.top_k(logits, K)
            neg_inf = jnp.full_like(logits, -jnp.inf)
            rows = jnp.arange(logits.shape[0])[:, None]
            masked = neg_inf.at[rows, top_idx].set(top_vals)
            return jax.nn.softmax(masked, axis=-1)
        gates = _gates(x[:, 0, :], Wr)
        mid = jnp.einsum('blh,erh->belr', x, A)
        expert_out = jnp.einsum('belr,ehr->belh', mid, Bw)
        weighted = jnp.einsum('be,belh->blh', gates, expert_out)
        return x + weighted

    def _L1_attn_ref(x, A_ssm, B_ssm, C_ssm, D_ssm, scale1, scale2, w1, b1, w2, b2):
        import jax, jax.numpy as jnp
        import numpy as np
        import math
        BATCH, SEQLEN, DMODEL, NSTATE, DFF = (4, 512, 256, 16, 1024)
        EPS = 1e-06

        def rmsnorm(x, scale):
            return x * jax.lax.rsqrt(jnp.mean(x * x, axis=-1, keepdims=True) + EPS) * scale

        def ssm_scan(u, A_ssm, B_ssm, C_ssm, D_ssm):
            dt = jnp.exp(jnp.linspace(math.log(0.001), math.log(0.1), NSTATE))
            expA = jnp.exp(A_ssm)
            dA = jnp.exp(-expA * dt)
            dB = B_ssm * (1.0 - dA) / expA

            def step(s, u_t):
                s = s * dA + u_t[..., None] * dB
                y = jnp.einsum('bdn,dn->bd', s, C_ssm)
                return (s, y)
            s0 = jnp.zeros((u.shape[0], DMODEL, NSTATE), dtype=u.dtype)
            _, ys = jax.lax.scan(step, s0, jnp.transpose(u, (1, 0, 2)))
            return jnp.transpose(ys, (1, 0, 2)) + u * D_ssm
        x = x + ssm_scan(rmsnorm(x, scale1), A_ssm, B_ssm, C_ssm, D_ssm)
        h = rmsnorm(x, scale2)
        h = jax.nn.gelu(h @ w1 + b1, approximate=False) @ w2 + b2
        return x + h

    def _L1_ffn_ref(x, ln1_g, ln1_b, Wqkv, Wproj, ln2_g, ln2_b, Wgate, W1, b1, W2, b2):
        import jax, jax.numpy as jnp
        import numpy as np
        import math
        B, T, D, H, E, TOPK, CAPF = (4, 512, 256, 16, 8, 2, 2.0)
        HD = D // H

        def layernorm(x, g, b, eps=1e-05):
            m = jnp.mean(x, -1, keepdims=True)
            v = jnp.mean(jnp.square(x - m), -1, keepdims=True)
            return (x - m) * jax.lax.rsqrt(v + eps) * g + b

        def block_forward(x, ln1_g, ln1_b, Wqkv, Wproj, ln2_g, ln2_b, Wgate, W1, b1, W2, b2):
            Bb, Tt, d = x.shape
            hd = HD
            half = hd // 2
            h = layernorm(x, ln1_g, ln1_b)
            qkv = (h @ Wqkv).reshape(Bb, Tt, H, 3 * hd)
            q, k, v = (qkv[..., :hd], qkv[..., hd:2 * hd], qkv[..., 2 * hd:])
            inv_freq = 1.0 / 10000.0 ** (jnp.arange(0, hd, 2, dtype=jnp.float32) / hd)
            ang = jnp.arange(Tt, dtype=jnp.float32)[:, None] * inv_freq
            sin = jnp.sin(ang)[None, :, None, :].astype(x.dtype)
            cos = jnp.cos(ang)[None, :, None, :].astype(x.dtype)

            def rope(t):
                t1, t2 = (t[..., :half], t[..., half:])
                return jnp.concatenate([t1 * cos - t2 * sin, t1 * sin + t2 * cos], -1)
            q, k = (rope(q), rope(k))
            scores = jnp.einsum('bqhd,bkhd->bhqk', q, k) / math.sqrt(hd)
            causal = jnp.tril(jnp.ones((Tt, Tt), dtype=bool))
            scores = jnp.where(causal, scores, jnp.asarray(-1000000000.0, scores.dtype))
            probs = jax.nn.softmax(scores, axis=-1)
            attn = jnp.einsum('bhqk,bkhd->bqhd', probs, v).reshape(Bb, Tt, d) @ Wproj
            x = x + attn
            h2 = layernorm(x, ln2_g, ln2_b)
            flat = h2.reshape(-1, d)
            N = flat.shape[0]
            capacity = int(math.ceil(CAPF * N / E))
            gates = jax.nn.softmax((flat @ Wgate).astype(jnp.float32), -1).astype(flat.dtype)
            _, top_inds = jax.lax.top_k(gates, TOPK)
            mask = jnp.zeros((N, E), dtype=bool).at[jnp.arange(N)[:, None], top_inds].set(True)
            pos = jnp.cumsum(mask.astype(jnp.int32), axis=0) * mask - 1
            keep = (pos < capacity) & mask
            t_flat = jnp.repeat(jnp.arange(N), TOPK)
            e_flat = top_inds.reshape(-1)
            p = pos[t_flat, e_flat]
            kp = keep[t_flat, e_flat]
            p_eff = jnp.where(kp, p, capacity)
            exp_in = jnp.zeros((E, capacity, d), flat.dtype).at[e_flat, p_eff].set(flat[t_flat], mode='drop')
            hmid = jax.nn.gelu(jnp.einsum('ecd,edf->ecf', exp_in, W1) + b1[:, None, :], approximate=False)
            exp_out = jnp.einsum('ecf,efd->ecd', hmid, W2) + b2[:, None, :]
            gate = gates[t_flat, e_flat] * kp.astype(flat.dtype)
            p_g = jnp.minimum(p_eff, capacity - 1)
            moe = jnp.zeros((N, d), flat.dtype).at[t_flat].add(exp_out[e_flat, p_g] * gate[:, None])
            return x + moe.reshape(Bb, Tt, d)
        return block_forward(x, ln1_g, ln1_b, Wqkv, Wproj, ln2_g, ln2_b, Wgate, W1, b1, W2, b2)
    x = L0_attn_x
    xn = _layernorm(x, axis=-1)
    s = _L0_attn_ref(xn, L0_attn_weight_q, L0_attn_weight_k, L0_attn_weight_v, L0_attn_theta)
    g = _silu(_L0_ffn_ref(xn, L0_ffn_Wr, L0_ffn_A, L0_ffn_Bw))
    x = x + s * g
    xn = _layernorm(x, axis=-1)
    s = _L1_attn_ref(xn, L1_attn_A_ssm, L1_attn_B_ssm, L1_attn_C_ssm, L1_attn_D_ssm, L1_attn_scale1, L1_attn_scale2, L1_attn_w1, L1_attn_b1, L1_attn_w2, L1_attn_b2)
    g = _silu(_L1_ffn_ref(xn, L1_ffn_ln1_g, L1_ffn_ln1_b, L1_ffn_Wqkv, L1_ffn_Wproj, L1_ffn_ln2_g, L1_ffn_ln2_b, L1_ffn_Wgate, L1_ffn_W1, L1_ffn_b1, L1_ffn_W2, L1_ffn_b2))
    x = x + s * g
    return x

_drawn_inputs = setup_inputs


def setup_inputs(seed=0):
    import zlib

    import numpy as np

    out = dict(_drawn_inputs(seed))
    spreads = {'L1_attn_D_ssm': (0.0, 0.1),
     'L1_attn_scale1': (1.0, 0.2),
     'L1_attn_scale2': (1.0, 0.6),
     'L1_attn_b1': (0.0, 0.702),
     'L1_attn_b2': (0.0, 0.1),
     'L1_ffn_ln1_g': (1.0, 0.6),
     'L1_ffn_ln1_b': (0.0, 0.8),
     'L1_ffn_ln2_g': (1.0, 0.6),
     'L1_ffn_ln2_b': (0.0, 0.8),
     'L1_ffn_b1': (0.0, 0.8),
     'L1_ffn_b2': (0.0, 2.0)}
    factors = {'L0_ffn_Wr': 4.797,
     'L0_ffn_A': 4.282,
     'L0_ffn_Bw': 4.308,
     'L1_ffn_Wqkv': 8.0,
     'L1_ffn_Wproj': 8.0,
     'L1_ffn_Wgate': 3.714,
     'L1_ffn_W1': 4.548,
     'L1_ffn_W2': 4.231}
    for name, (base, spread) in spreads.items():
        noise = np.random.default_rng([zlib.crc32(name.encode()), seed]).standard_normal(out[name].shape)
        drawn = base * np.exp(spread * noise) if base else spread * noise
        out[name] = jnp.asarray(drawn.astype(out[name].dtype))
    for name, factor in factors.items():
        out[name] = (out[name] * factor).astype(out[name].dtype)
    return out
```

```python
from contextlib import ExitStack

import concourse.bass as bass
from concourse import mybir

F32 = mybir.dt.float32
BF16 = mybir.dt.bfloat16
I32 = mybir.dt.int32
F22 = mybir.dt.float32r
ALU = mybir.AluOpType
ACT = mybir.ActivationFunctionType
AX_X = mybir.AxisListType.X

P = 128
B, L, D = 8, 1024, 256
N = B * L
CH = L // P
TILES = N // P
E0, R0 = 8, 64
NST = 16
G = D // 4
EXPERTS, CAP = 8, 2 * N // 8
NH, HD = 16, 16
GAMMA = 0.96875
LN_EPS, RMS_EPS = 1e-5, 1e-6



def high_part(nc, out, x):
    return nc.vector.tensor_copy(out, x)


def low_part(nc, out, x, high):
    return nc.vector.tensor_tensor(out, x, high.bitcast(F32), ALU.subtract)


def wait_apart(eng, sem, count, passed):
    eng.wait_ge(sem, count)
    if not isinstance(count, int):
        eng.sem_inc(passed, 1)


def need(eng, sem, count):
    if not isinstance(count, int) or count > 0:
        eng.wait_ge(sem, count)


SCRATCH = {
    "x1": ((N, D), F32),
    "moments1": ((P, TILES * 2), F32),
    "z_row": ((D, 32), F32),
    "kpad": ((D, 2 * P), F32),
    "xa": ((N, D), F32),
    "moments_a": ((P, TILES * 2), F32),
    "s1": ((N, D), F32),
    "v": ((N, D), F32),
    "parts": ((6, D, N), BF16),
    "attn": ((N, D), F32),
    "x2": ((N, D), F32),
    "slots": ((P, TILES * 2), I32),
    "weights": ((P, TILES * 2), F32),
    "expert_in": ((EXPERTS * CAP, D), F32),
    "expert_out": ((EXPERTS * CAP, D), F32),
}


def constants():
    import numpy as np

    c = {}
    c["ident"] = np.eye(P, dtype=np.float32)
    step = np.arange(P)
    g = GAMMA ** np.arange(-P, P + 1, dtype=np.float64)
    c["decay_mask"] = np.where(step[None] >= step[:, None], g[P - 1 - step][:, None], 0.0).astype(np.float32)
    c["decay_row"] = np.tile(g[P + 1 + step][None], (P, 1)).astype(np.float32)
    c["decay_col"] = g[P + P - 1 - step][:, None].astype(np.float32)
    rows = np.zeros((E0, 4 * P), np.float32)
    rows[np.arange(4 * P) // R0, np.arange(4 * P)] = 1.0
    c["expert_rows"] = rows
    dt = np.exp(np.linspace(np.log(0.001), np.log(0.1), NST)).astype(np.float32)
    c["dt_row"] = np.tile(dt[None], (P, 1))
    c["lags"] = np.tile(np.arange(P + 1, dtype=np.float32)[None], (P, 1))
    c["neg_left"] = -(P - 1 - step)[:, None].astype(np.float32)
    c["quad_ones"] = (step[:, None] // 32 == np.arange(4)[None]).astype(np.float32)
    inv_freq = (1.0 / 10000.0 ** (np.arange(0, HD, 2, dtype=np.float32) / HD)).astype(np.float32)
    ang = np.arange(L, dtype=np.float32)[:, None] * inv_freq
    cos, sin = np.cos(ang), np.sin(ang)
    tabs = []
    for t in (np.concatenate([cos, cos], 1), np.concatenate([-sin, sin], 1)):
        t = np.stack([t * np.float32(HD ** -0.5), t], 1)
        tabs.append(t.reshape(CH, P, 2 * HD).transpose(1, 0, 2).reshape(P, CH * 2 * HD).astype(np.float32))
    c["rope_c"], c["rope_s"] = tabs
    c["tri_ones"] = np.triu(np.ones((P, P), np.float32))
    c["ones"] = np.ones((P, P), np.float32)
    expert = np.arange(EXPERTS)
    c["lower"] = np.tile((expert[None] < expert[:, None]).astype(np.float32).reshape(1, -1), (P, 1))
    c["slot_base"] = np.tile((expert * CAP - 1).astype(np.float32)[None], (P, 1))
    later = np.where(step[None] > step[:, None], -1e30, 0.0).astype(np.float32)
    c["masks"] = np.concatenate([later, later.T], 1)
    return c


def phase_l0(nc, ctx, d):
    with ExitStack() as mem:
        def sb(name, shape, dt=F32):
            return mem.enter_context(nc.sbuf_tensor("l0_" + name, shape, dt))

        def sem(name):
            return ctx.enter_context(nc.semaphore("l0_" + name))

        bank = [mem.enter_context(nc.psum_tensor(f"l0_bank{i}", [P, 512], F32)) for i in range(8)]

        ident = sb("ident", [P, P])
        x_all = sb("x_all", [P, TILES, D])
        stats = sb("stats", [P, TILES, 6])
        moments = sb("moments", [P, TILES, 2])
        moments1 = sb("moments1", [P, TILES, 2])
        rstd = sb("rstd", [P, TILES])
        var_eps = sb("var_eps", [P, TILES])
        minus_half = sb("minus_half", [P, TILES])
        decay_mask = sb("decay_mask", [P, P])
        decay_row = sb("decay_row", [P, P])
        decay_col = sb("decay_col", [P, 1])
        cls = sb("cls", [B, D])
        cls_n = sb("cls_n", [B, D])
        cls_stats = sb("cls_stats", [B, 6])
        cls_mom = sb("cls_mom", [B, 2])
        cls_rstd = sb("cls_rstd", [B, 1])
        wr = sb("wr", [E0, D])
        wr_t = sb("wr_t", [P, 2, E0])
        cls_t = sb("cls_t", [P, 2, B])
        logits = sb("logits", [B, E0])
        beats = sb("beats", [B, E0])
        rank = sb("rank", [B, E0])
        neg_max = sb("neg_max", [B, 1])
        gate_e = sb("gate_e", [B, E0])
        gate_s = sb("gate_s", [B, E0])
        gate_sum = sb("gate_sum", [B, 1])
        gates = sb("gates", [B, E0])
        gates_t = sb("gates_t", [E0, B])
        expert_rows = sb("expert_rows", [E0, 4, P])
        gate_col = sb("gate_col", [P, 4, B])
        a_nat = sb("a_nat", [P, 4, D])
        bw_nat = sb("bw_nat", [P, 2, E0 * R0])
        bw_t = sb("bw_t", [P, 4, D])
        bw_g = sb("bw_g", [P, 2, 4, D])
        mix_w = sb("mix_w", [P, B, 2, D])
        wq = sb("wq", [P, 2, D])
        wk = sb("wk", [P, 2, D])
        wv = sb("wv", [P, 2, D])
        wq_t = sb("wq_t", [P, 2, D])
        wk_t = sb("wk_t", [P, 2, D])
        theta = sb("theta", [P, 2])
        thetas = sb("thetas", [P, 2])
        g_qk = sb("g_qk", [P, 2, D])
        xn = sb("xn", [P, 2, D])
        xn_d = sb("xn_d", [P, 2, D])
        xn_t = sb("xn_t", [P, 4, 2, P])
        q_d = sb("q_d", [P, 2, 2, P])
        v = sb("v", [P, 2, D])
        gate = sb("gate", [P, 2, D])
        s_m = sb("s_m", [P, 2, P])
        sg = sb("sg", [P, 2, D])
        state = sb("state", [P, 2, 2, D])

        s_const, s_gw, s_qk, s_x = sem("const"), sem("gate_weights"), sem("qk_weights"), [sem(f"x_in{b}") for b in range(B)]
        s_dve, s_act, s_pe, s_pool = sem("dve_step"), sem("act_step"), sem("pe_step"), sem("pool_step")
        s_cls = sem("class_rows")
        s_rstd_in, s_rstd = sem("var_ready"), sem("rstd_ready")
        s_stat = sem("stats_ready")
        s_mixs, s_mixp, s_mixw = sem("mix_scaled"), sem("mix_product"), sem("mix_ready")
        c_xn, c_xnd, c_xt, c_xnt = sem("xn"), sem("xn_decayed"), sem("xt_psum"), sem("xn_t")
        c_q, c_qd, c_s, c_sm = sem("q_psum"), sem("q_decayed"), sem("scores"), sem("scores_masked")
        c_vg, c_v, c_gate = sem("vg_psum"), sem("v"), sem("gate")
        c_st, c_state, c_out, c_sg, c_x1 = sem("state_psum"), sem("state"), sem("out_psum"), sem("sg"), sem("x1")
        c_stat, c_mom, s_done = sem("x1_stats"), sem("x1_moments"), sem("stored")

        vg_bank = [bank[3], bank[6]]
        block = mem.enter_context(nc.Block())
        x_d = d["L0_attn_x"].rearrange("b (c p) h -> b p c h", p=P)
        x1_d = d["x1"].rearrange("(t p) h -> p t h", p=P)

        def at(b, c, o):
            b2, c2 = b + (c + o) // CH, (c + o) % CH
            return None if isinstance(b2, int) and b2 >= B else (b2, c2)

        def chunks(eng, turn):
            for c in range(CH):
                turn(0, c)
            with eng.Fori(1, B - 1) as b:
                for c in range(CH):
                    turn(b, c)
            for c in range(CH):
                turn(B - 1, c)

        @block.sync
        def _(sp):
            sp.dma_start(ident[:, :], d["ident"]).then_inc(s_const, 16)
            sp.dma_start(cls[:, :], d["L0_attn_x"][:, 0, :]).then_inc(s_cls, 16)
            sp.dma_start(wr[:, :], d["L0_ffn_Wr"]).then_inc(s_cls, 16)
            for k in range(2):
                sp.dma_start(bw_nat[:, k, :].rearrange("p (e r) -> p e r", r=R0),
                             d["L0_ffn_Bw"][:, k * P:(k + 1) * P, :].rearrange("e p r -> p e r")).then_inc(s_gw, 16)
            sp.dma_start(a_nat[:, :, :], d["L0_ffn_A"].rearrange("(c e) r h -> (e r) c h", e=2)).then_inc(s_gw, 16)
            for b in range(B):
                sp.dma_start(x_all[:, b * CH:(b + 1) * CH, :], x_d[b]).then_inc(s_x[b], 16)
            with sp.Fori(0, B) as b:
                sp.wait_ge(c_x1, b * CH + CH)
                sp.dma_start(x1_d[:, bass.ts(b, CH), :], x_all[:, bass.ts(b, CH), :]).then_inc(s_done, 16)
            sp.wait_ge(c_mom, TILES)
            sp.dma_start(d["moments1"].rearrange("p (t k) -> p t k", k=2), moments1[:, :, :]).then_inc(s_done, 16)
            sp.wait_ge(s_done, 16 * (B + 1))

        @block.gpsimd
        def _(pool):
            nc.gpsimd.memset(minus_half[:, :], -0.5).then_inc(s_pool, 1)
            pool.wait_ge(s_pool, 1)
            pool.wait_ge(s_rstd_in, 1)
            nc.gpsimd.tensor_tensor(cls_rstd[:, :], cls_rstd[:, :], minus_half[0:B, 0:1], ALU.pow).then_inc(s_rstd, 1)
            pool.wait_ge(s_rstd_in, 2)
            nc.gpsimd.tensor_tensor(rstd[:, :], var_eps[:, :], minus_half[:, :], ALU.pow).then_inc(s_rstd, 1)
            pool.wait_ge(s_const, 80)
            def decay_keys(b, c):
                pool.wait_ge(c_xn, b * CH + c + 1)
                need(pool, c_st, b * (CH - 1) + max(c - 1, 0))
                nc.gpsimd.tensor_tensor(xn_d[:, c % 2], xn[:, c % 2], decay_col[:, 0:1].to_broadcast([P, D]), ALU.mult).then_inc(c_xnd, 1)

            def turn(b, c):
                nxt = at(b, c, 2)
                if nxt and nxt[1] < CH - 1:
                    decay_keys(*nxt)
                k = b * CH + c
                pool.wait_ge(c_sg, k + 1)
                nc.gpsimd.tensor_tensor(x_all[:, k, :], x_all[:, k, :], sg[:, c % 2], ALU.add).then_inc(c_x1, 1)

            decay_keys(0, 0)
            decay_keys(0, 1)
            chunks(pool, turn)

        @block.scalar
        def _(act):
            act.dma_start(decay_mask[:, :], d["decay_mask"]).then_inc(s_const, 16)
            act.dma_start(decay_row[:, :], d["decay_row"]).then_inc(s_const, 16)
            act.dma_start(decay_col[:, :], d["decay_col"]).then_inc(s_const, 16)
            act.dma_start(expert_rows[:, :, :], d["expert_rows"].rearrange("e (c p) -> e c p", p=P)).then_inc(s_const, 16)
            act.dma_start(wq[:, :, :], d["L0_attn_weight_q"].rearrange("(k p) n -> p k n", p=P)).then_inc(s_qk, 16)
            act.dma_start(wk[:, :, :], d["L0_attn_weight_k"].rearrange("(k p) n -> p k n", p=P)).then_inc(s_qk, 16)
            act.dma_start(wv[:, :, :], d["L0_attn_weight_v"].rearrange("(k p) n -> p k n", p=P)).then_inc(s_qk, 16)
            with nc.allow_non_contiguous_dma(reason="256 angles, once"):
                act.dma_start(theta[:, :], d["L0_attn_theta"].rearrange("(k p) -> p k", p=P)).then_inc(s_qk, 16)
            act.wait_ge(s_qk, 64)
            nc.scalar.activation(thetas[:, :], theta[:, :], ACT.Exp, scale=0.0).then_inc(s_act, 1)
            act.wait_ge(s_act, 1)
            act.wait_ge(s_pe, 1)
            for k in range(2):
                ins = nc.scalar.activation(wq_t[:, k, :], bank[0][:, k * D:(k + 1) * D], ACT.Copy, scale=thetas[:, k:k + 1])
            ins.then_inc(s_act, 1)
            act.wait_ge(s_pe, 2)
            for k in range(2):
                ins = nc.scalar.activation(wk_t[:, k, :], bank[1][:, k * D:(k + 1) * D], ACT.Copy, scale=thetas[:, k:k + 1])
            ins.then_inc(s_act, 1)
            act.wait_ge(s_pe, 3)
            nc.scalar.activation(g_qk[:, :, :], bank[2][:, :].rearrange("p (k n) -> p k n", k=2), ACT.Copy).then_inc(s_act, 1)
            act.wait_ge(s_pe, 4)
            nc.scalar.activation(bw_t[:, 0:2, :], bank[3][:, :].rearrange("p (k n) -> p k n", k=2), ACT.Copy)
            nc.scalar.activation(bw_t[:, 2:4, :], bank[4][:, :].rearrange("p (k n) -> p k n", k=2), ACT.Copy).then_inc(s_act, 1)
            act.wait_ge(s_dve, 5)
            nc.scalar.activation(gate_e[:, :], logits[:, :], ACT.Exp, bias=neg_max[:, 0:1]).then_inc(s_act, 1)
            def take_turned(b, c):
                act.wait_ge(c_xt, b * CH + c + 1)
                nc.scalar.activation(xn_t[:, c % 4], bank[0][:, 0:D].rearrange("p (k n) -> p k n", k=2), ACT.Identity).then_inc(c_xnt, 1)

            def take_v_and_gate(b, c):
                k, n = b * CH + c, c % 2
                act.wait_ge(c_vg, k + 1)
                nc.scalar.activation(v[:, n], vg_bank[n][:, 0:D], ACT.Identity).then_inc(c_v, 1)
                need(act, c_sg, k - 1)
                nc.scalar.activation(gate[:, n], vg_bank[n][:, D:2 * D], ACT.Silu).then_inc(c_gate, 1)

            def turn(b, c):
                if at(b, c, 2):
                    take_turned(*at(b, c, 2))
                if at(b, c, 1):
                    take_v_and_gate(*at(b, c, 1))

            take_turned(0, 0)
            take_turned(0, 1)
            take_v_and_gate(0, 0)
            chunks(act, turn)

        @block.vector
        def _(dve):
            dve.wait_ge(s_cls, 32)
            nc.vector.bn_stats(cls_stats[:, :], cls[:, :]).then_inc(s_stat, 1)
            dve.wait_ge(s_stat, 1)
            nc.vector.bn_aggr(cls_mom[:, :], cls_stats[:, :]).then_inc(s_stat, 1)
            dve.wait_ge(s_stat, 2)
            nc.vector.tensor_scalar(cls_rstd[:, :], cls_mom[:, 1:2], LN_EPS, None, ALU.add).then_inc(s_rstd_in, 1)
            dve.wait_ge(s_rstd, 1)
            nc.vector.tensor_scalar(cls_n[:, :], cls[:, :], cls_mom[:, 0:1], cls_rstd[:, 0:1], ALU.subtract, ALU.mult).then_inc(s_dve, 1)
            dve.wait_ge(s_pe, 5)
            nc.vector.tensor_copy(cls_t[:, :, :], bank[5][:, 0:2 * B].rearrange("p (k n) -> p k n", k=2)).then_inc(s_dve, 1)
            nc.vector.tensor_copy(wr_t[:, :, :], bank[5][:, 2 * B:2 * B + 2 * E0].rearrange("p (k n) -> p k n", k=2)).then_inc(s_dve, 1)
            dve.wait_ge(s_pe, 6)
            nc.vector.tensor_copy(logits[:, :], bank[6][0:B, 0:E0]).then_inc(s_dve, 1)
            dve.wait_ge(s_dve, 4)
            nc.vector.tensor_reduce(neg_max[:, :], logits[:, :], AX_X, ALU.max, negate=True).then_inc(s_dve, 1)
            nc.vector.memset(rank[:, :], 0.0).then_inc(s_stat, 1)
            step = 3
            for e in range(E0):
                dve.wait_ge(s_stat, step)
                if e > 0:
                    nc.vector.tensor_scalar(beats[:, 0:e], logits[:, 0:e], logits[:, e:e + 1], None, ALU.is_lt)
                ins = nc.vector.tensor_scalar(beats[:, e:E0], logits[:, e:E0], logits[:, e:e + 1], None, ALU.is_le)
                ins.then_inc(s_stat, 1)
                dve.wait_ge(s_stat, step + 1)
                nc.vector.tensor_tensor(rank[:, :], rank[:, :], beats[:, :], ALU.add).then_inc(s_stat, 1)
                step += 2
            dve.wait_ge(s_stat, step)
            dve.wait_ge(s_act, 6)
            nc.vector.scalar_tensor_tensor(gate_s[:, :], rank[:, :], 2.5, gate_e[:, :], ALU.is_lt, ALU.mult).then_inc(s_dve, 1)
            dve.wait_ge(s_dve, 6)
            nc.vector.tensor_reduce(gate_sum[:, :], gate_s[:, :], AX_X, ALU.add).then_inc(s_dve, 1)
            dve.wait_ge(s_dve, 7)
            nc.vector.reciprocal(gate_sum[:, :], gate_sum[:, :]).then_inc(s_dve, 1)
            dve.wait_ge(s_dve, 8)
            nc.vector.tensor_scalar(gates[:, :], gate_s[:, :], gate_sum[:, 0:1], None, ALU.mult).then_inc(s_dve, 1)
            dve.wait_ge(s_pe, 7)
            nc.vector.tensor_copy(gates_t[:, :], bank[5][0:E0, 0:B]).then_inc(s_dve, 1)
            dve.wait_ge(s_pe, 8)
            nc.vector.tensor_copy(gate_col[:, :, :], bank[6][:, 0:4 * B].rearrange("p (c b) -> p c b", b=B)).then_inc(s_dve, 1)
            dve.wait_ge(s_dve, 11)
            for b in range(B):
                if b >= 2:
                    dve.wait_ge(s_mixp, b - 1)
                for c in range(4):
                    ins = nc.vector.tensor_scalar(bw_g[:, b % 2, c, :], bw_t[:, c, :], gate_col[:, c, b:b + 1], None, ALU.mult)
                ins.then_inc(s_mixs, 1)
                dve.wait_ge(s_x[b], 16)
                for t in range(b * CH, (b + 1) * CH):
                    nc.vector.bn_stats(stats[:, t, :], x_all[:, t, :]).then_inc(s_stat, 1)
                if b >= 1:
                    dve.wait_ge(s_mixp, b)
                    nc.vector.tensor_copy(mix_w[:, b - 1], bank[(b - 1) % 2][:, :].rearrange("p (k n) -> p k n", k=2)).then_inc(s_mixw, 1)
            dve.wait_ge(s_mixp, B)
            nc.vector.tensor_copy(mix_w[:, B - 1], bank[(B - 1) % 2][:, :].rearrange("p (k n) -> p k n", k=2)).then_inc(s_mixw, 1)
            dve.wait_ge(s_mixw, B)
            for k in range(2):
                sl = mix_w[:, :, k, k * P:(k + 1) * P]
                ins = nc.vector.tensor_tensor(sl, sl, ident[:, :].unsqueeze(1).to_broadcast([P, B, P]), ALU.add)
            ins.then_inc(s_mixw, 1)
            dve.wait_ge(s_stat, step + TILES)
            for t in range(TILES):
                nc.vector.bn_aggr(moments[:, t, :], stats[:, t, :]).then_inc(s_stat, 1)
            dve.wait_ge(s_stat, step + 2 * TILES)
            nc.vector.tensor_scalar(var_eps[:, :], moments[:, :, 1], LN_EPS, None, ALU.add).then_inc(s_rstd_in, 1)
            dve.wait_ge(s_rstd, 2)
            def normalise(b, c):
                k, n = b * CH + c, c % 2
                need(dve, c_xt, k - 1)
                need(dve, c_xnd, b * (CH - 1) + max(c - 1, 0))
                nc.vector.tensor_scalar(xn[:, n], x_all[:, k, :], moments[:, k, 0:1],
                                        rstd[:, bass.ds(k, 1)], ALU.subtract, ALU.mult).then_inc(c_xn, 1)

            def decay_q(b, c):
                dve.wait_ge(c_q, b * CH + c + 1)
                nc.vector.tensor_tensor(q_d[:, c % 2], bank[1][:, 0:D].rearrange("p (k n) -> p k n", k=2),
                                        decay_row[:, :].unsqueeze(1).to_broadcast([P, 2, P]), ALU.mult).then_inc(c_qd, 1)

            def x1_statistics(b, c):
                k = b * CH + c
                dve.wait_ge(c_x1, k + 1)
                nc.vector.bn_stats(stats[:, k, :], x_all[:, k, :]).then_inc(c_stat, 1)

            def turn(b, c):
                k, n = b * CH + c, c % 2
                if at(b, c, 1):
                    decay_q(*at(b, c, 1))
                dve.wait_ge(c_s, k + 1)
                nc.vector.tensor_tensor(s_m[:, n], bank[2][:, 0:P], decay_mask[:, :], ALU.mult).then_inc(c_sm, 1)
                if at(b, c, 3):
                    normalise(*at(b, c, 3))
                if c + 1 < CH:
                    dve.wait_ge(c_st, b * (CH - 1) + c + 1)
                    new = bank[5][:, :].rearrange("p (k n) -> p k n", k=2)
                    if c == 0:
                        nc.vector.tensor_copy(state[:, 0], new).then_inc(c_state, 1)
                    else:
                        dve.wait_ge(c_state, b * (CH - 1) + c)
                        nc.vector.scalar_tensor_tensor(state[:, n], state[:, 1 - n], GAMMA ** P, new, ALU.mult, ALU.add).then_inc(c_state, 1)
                if not (isinstance(b, int) and k < 1):
                    x1_statistics(*((b, c - 1) if c else (b - 1, CH - 1)))
                dve.wait_ge(c_out, k + 1)
                dve.wait_ge(c_gate, k + 1)
                need(dve, c_x1, k - 1)
                nc.vector.tensor_tensor(sg[:, n], bank[4][:, 0:D], gate[:, n], ALU.mult).then_inc(c_sg, 1)

            for c in range(3):
                normalise(0, c)
            decay_q(0, 0)
            chunks(dve, turn)
            x1_statistics(B - 1, CH - 1)
            for t in range(TILES):
                if t == 0:
                    dve.wait_ge(c_stat, TILES)
                nc.vector.bn_aggr(moments1[:, t, :], stats[:, t, :]).then_inc(c_mom, 1)

        @block.tensor
        def _(pe):
            pe.wait_ge(s_const, 80)
            pe.wait_ge(s_qk, 64)
            for w, o in ((wq, 0), (wk, 1)):
                for i in range(2):
                    for j in range(2):
                        ins = nc.tensor.transpose(bank[o][:, j * D + i * P:j * D + (i + 1) * P], w[:, i, j * P:(j + 1) * P], ident[:, :])
                ins.then_inc(s_pe, 1)
            pe.wait_ge(s_act, 3)
            for i in range(2):
                for k in range(2):
                    ins = nc.tensor.matmul(bank[2][:, i * D:(i + 1) * D], wq_t[:, k, i * P:(i + 1) * P], wk_t[:, k, :], start=(k == 0), stop=(k == 1))
            ins.then_inc(s_pe, 1)
            pe.wait_ge(s_gw, 48)
            for c in range(4):
                for k in range(2):
                    ins = nc.tensor.transpose(bank[3 + c // 2][:, (c % 2) * D + k * P:(c % 2) * D + (k + 1) * P], bw_nat[:, k, c * P:(c + 1) * P], ident[:, :])
            ins.then_inc(s_pe, 1)
            pe.wait_ge(s_dve, 1)
            for k in range(2):
                nc.tensor.transpose(bank[5][:, k * B:(k + 1) * B], cls_n[:, k * P:(k + 1) * P], ident[0:B, 0:B])
            for k in range(2):
                ins = nc.tensor.transpose(bank[5][:, 2 * B + k * E0:2 * B + (k + 1) * E0], wr[:, k * P:(k + 1) * P], ident[0:E0, 0:E0])
            ins.then_inc(s_pe, 1)
            pe.wait_ge(s_dve, 3)
            for k in range(2):
                ins = nc.tensor.matmul(bank[6][0:B, 0:E0], cls_t[:, k, :], wr_t[:, k, :], start=(k == 0), stop=(k == 1))
            ins.then_inc(s_pe, 1)
            pe.wait_ge(s_dve, 9)
            nc.tensor.transpose(bank[5][0:E0, 0:B], gates[:, :], ident[0:B, 0:B]).then_inc(s_pe, 1)
            pe.wait_ge(s_dve, 10)
            for c in range(4):
                ins = nc.tensor.matmul(bank[6][:, c * B:(c + 1) * B], expert_rows[:, c, :], gates_t[:, :], start=True, stop=True)
            ins.then_inc(s_pe, 1)
            for b in range(B):
                pe.wait_ge(s_mixs, b + 1)
                if b >= 2:
                    pe.wait_ge(s_mixw, b - 1)
                for i in range(2):
                    for c in range(4):
                        ins = nc.tensor.matmul(bank[b % 2][:, i * D:(i + 1) * D], a_nat[:, c, i * P:(i + 1) * P], bw_g[:, b % 2, c, :], start=(c == 0), stop=(c == 3))
                ins.then_inc(s_mixp, 1)
            pe.wait_ge(s_mixw, B + 1)
            pe.wait_ge(s_act, 4)
            def turn_rows(b, c):
                k = b * CH + c
                pe.wait_ge(c_xn, k + 1)
                need(pe, c_xnt, k)
                for i in range(2):
                    ins = nc.tensor.transpose(bank[0][:, i * P:(i + 1) * P], xn[:, c % 2, i * P:(i + 1) * P], ident[:, :])
                ins.then_inc(c_xt, 1)

            def project_q(b, c):
                k = b * CH + c
                pe.wait_ge(c_xnt, k + 1)
                need(pe, c_qd, k)
                for j in range(2):
                    for i in range(2):
                        ins = nc.tensor.matmul(bank[1][:, j * P:(j + 1) * P], g_qk[:, i, j * P:(j + 1) * P], xn_t[:, c % 4, i, :], start=(i == 0), stop=(i == 1))
                ins.then_inc(c_q, 1)

            def project_v_and_gate(b, c):
                out = vg_bank[c % 2]
                need(pe, c_gate, b * CH + c - 1)
                for i in range(2):
                    nc.tensor.matmul(out[:, 0:D], xn_t[:, c % 4, i, :], wv[:, i, :], start=(i == 0), stop=(i == 1))
                for i in range(2):
                    ins = nc.tensor.matmul(out[:, D:2 * D], xn_t[:, c % 4, i, :], mix_w[:, b, i, :], start=(i == 0), stop=(i == 1))
                ins.then_inc(c_vg, 1)

            def turn(b, c):
                k, n = b * CH + c, c % 2
                if at(b, c, 2):
                    turn_rows(*at(b, c, 2))
                if at(b, c, 1):
                    project_q(*at(b, c, 1))
                pe.wait_ge(c_qd, k + 1)
                need(pe, c_sm, k)
                for i in range(2):
                    ins = nc.tensor.matmul(bank[2][:, 0:P], xn_t[:, c % 4, i, :], q_d[:, n, i, :], start=(i == 0), stop=(i == 1))
                ins.then_inc(c_s, 1)
                e = b * (CH - 1) + c
                if c + 1 < CH:
                    pe.wait_ge(c_v, k + 1)
                    need(pe, c_state, e)
                    pe.wait_ge(c_xnd, e + 1)
                    for i in range(2):
                        ins = nc.tensor.matmul(bank[5][:, i * D:(i + 1) * D], xn_d[:, n, i * P:(i + 1) * P], v[:, n], start=True, stop=True)
                    ins.then_inc(c_st, 1)
                if at(b, c, 1):
                    project_v_and_gate(*at(b, c, 1))
                pe.wait_ge(c_sm, k + 1)
                need(pe, c_sg, k)
                if c + 1 == CH:
                    pe.wait_ge(c_v, k + 1)
                    pe.wait_ge(c_state, e)
                ins = nc.tensor.matmul(bank[4][:, 0:D], s_m[:, n], v[:, n], start=True, stop=(c == 0))
                if c >= 1:
                    for i in range(2):
                        ins = nc.tensor.matmul(bank[4][:, 0:D], q_d[:, n, i, :], state[:, 1 - n, i, :], start=False, stop=(i == 1))
                ins.then_inc(c_out, 1)

            turn_rows(0, 0)
            turn_rows(0, 1)
            project_q(0, 0)
            project_v_and_gate(0, 0)
            chunks(pe, turn)


def phase_ssm(nc, ctx, d):
    with ExitStack() as mem:
        def sb(name, shape, dt=F32):
            return mem.enter_context(nc.sbuf_tensor("ssm_" + name, shape, dt))

        def sem(name):
            return ctx.enter_context(nc.semaphore("ssm_" + name))

        bank = [mem.enter_context(nc.psum_tensor(f"ssm_bank{i}", [P, 512], F32)) for i in range(8)]

        ident = sb("ident", [P, P])
        u = sb("u", [P, TILES, D])
        mom = sb("mom", [P, TILES, 2])
        rstd = sb("rstd", [P, TILES])
        rms = sb("rms", [P, TILES])
        small = sb("small", [P, TILES])
        minus_half = sb("minus_half", [P, TILES])
        a_nat = sb("a_nat", [P, 2, NST])
        b_nat = sb("b_nat", [P, 2, NST])
        c_nat = sb("c_nat", [P, 2, NST])
        scale_nat = sb("scale_nat", [P, 2])
        dt_row = sb("dt_row", [P, NST])
        exp_a = sb("exp_a", [P, 2, NST])
        th = sb("th", [P, 2, NST])
        th1 = sb("th1", [P, 2, NST])
        z4 = sb("z4", [P, 2, 4, 32])
        c4 = sb("c4", [P, 2, 4, 32])
        z_t = sb("z_t", [P, G])
        c_t = sb("c_t", [P, G])
        w128 = sb("w128", [P, G])
        lags = sb("lags", [P, P + 1])
        powers = sb("powers", [P, G, P + 1])
        neg_left = sb("neg_left", [P, 1])
        back = sb("back", [P, D, 32])
        quad_ones = sb("quad_ones", [P, 4])
        d4 = sb("d4", [4, G])
        s4 = sb("s4", [4, G])
        kern = sb("kern", [4, 2, 4, P])
        zeros = sb("zeros", [P, D])
        state = sb("state", [P, G, B, CH])
        carry = sb("carry", [P, G, B])
        NT = 4
        hankel = [sb(f"hankel{i}", [P, 4, P]) for i in range(NT)]
        toep = [sb(f"toep{i}", [P, 4, P]) for i in range(2)]
        NX = 8
        x_in = sb("x_in", [P, NX, D * 4])
        bias = sb("bias", [P, TILES])
        st = sb("st", [P, TILES, 6])
        mom_out = sb("mom_out", [P, TILES, 2])

        s_in, s_x, s_act, s_dve, s_pool = sem("in"), [sem(f"x_in{b}") for b in range(B)], sem("act"), sem("dve"), sem("pool")
        s_pe, s_z, s_zb = sem("pe"), sem("zeros_kernel"), sem("z_broadcast")
        s_pwz, s_pwe, s_pw = sem("lag_exponents"), sem("lag_powers"), sem("lag_weights")
        s_kp, s_ks, s_kd, s_kz = sem("kernel_psum"), sem("kernel_taken"), sem("kernel_added"), [sem("kernel_stored0"), sem("kernel_stored1")]
        s_u, s_back = sem("u"), sem("back")
        s_sl, s_sle, s_scan = sem("local_states"), sem("local_states_kept"), sem("scan")
        s_t, s_flip = [sem(f"hankel{i}") for i in range(NT)], sem("toep")
        s_y, s_ye = sem("y"), sem("y_kept")
        s_xr = [sem(f"x_again{n}") for n in range(NX)]
        s_xn, s_xa, s_stat, s_out, s_mo = sem("xn"), sem("xa"), sem("stat"), [sem(f"xa_stored{n}") for n in range(NX)], sem("moments_stored")
        s_pst, s_bias = sem("pool_start"), sem("bias")

        block = mem.enter_context(nc.Block())
        x1_d = d["x1"].rearrange("(t p) h -> p t h", p=P)
        x1_q = d["x1"].rearrange("(q t p) h -> q p t h", p=P, t=4)
        xa_q = d["xa"].rearrange("(q t p) h -> q p t h", p=P, t=4)
        kpad = d["kpad"]
        Q = TILES // 4

        @block.sync
        def _(sp):
            for dst, src in ((ident[:, :], d["ident"]), (mom[:, :, :], d["moments1"].rearrange("p (t k) -> p t k", k=2)),
                             (a_nat[:, :, :], d["L1_attn_A_ssm"].rearrange("(k p) n -> p k n", p=P)),
                             (b_nat[:, :, :], d["L1_attn_B_ssm"].rearrange("(k p) n -> p k n", p=P)),
                             (c_nat[:, :, :], d["L1_attn_C_ssm"].rearrange("(k p) n -> p k n", p=P)),
                             (dt_row[:, :], d["dt_row"]), (lags[:, :], d["lags"]), (neg_left[:, :], d["neg_left"]),
                             (quad_ones[:, :], d["quad_ones"]),
                             (d4[:, :], d["L1_attn_D_ssm"].rearrange("(i g) -> i g", i=4)),
                             (s4[:, :], d["L1_attn_scale1"].rearrange("(i g) -> i g", i=4))):
                sp.dma_start(dst, src).then_inc(s_in, 16)
            with nc.allow_non_contiguous_dma(reason="256 scales, once"):
                sp.dma_start(scale_nat[:, :], d["L1_attn_scale1"].rearrange("(k p) -> p k", p=P)).then_inc(s_in, 16)
            for b in range(B):
                sp.dma_start(u[:, b * CH:(b + 1) * CH, :], x1_d[:, b * CH:(b + 1) * CH, :]).then_inc(s_x[b], 16)
            sp.wait_ge(s_act, 3)
            for k in range(2):
                sp.dma_start(d["z_row"][k * P:(k + 1) * P, :], z4[:, k, 0, :]).then_inc(s_zb, 16)
            sp.wait_ge(s_zb, 32)
            sp.dma_start(back[:, :, :].rearrange("p a b -> p (a b)"),
                         d["z_row"].rearrange("a b -> (a b)").unsqueeze(0).to_broadcast([P, D * 32])).then_inc(s_zb, 16)
            sp.wait_ge(s_pool, 1)
            sp.dma_start(kpad[:, P:2 * P].rearrange("(k p) t -> p k t", p=P), zeros[:, :].rearrange("p (k t) -> p k t", k=2)).then_inc(s_z, 16)
            kp = kpad[:, 0:P].rearrange("(i g) t -> i g t", i=4)
            for m in range(G // 4):
                sp.wait_ge(s_kd, m + 1)
                sp.dma_start(kp[:, 4 * m:4 * m + 4, :], kern[:, m % 2]).then_inc(s_kz[m % 2], 16)
            sp.wait_ge(s_z, 16)
            for h in range(2):
                sp.wait_ge(s_kz[h], 16 * G // 8)
            for g in range(G):
                if g >= NT:
                    sp.wait_ge(s_flip, g - NT + 1)
                src = bass.AP(kpad.tensor, g * 2 * P, [[1, P], [G * 2 * P, 4], [1, P]])
                sp.dma_start(hankel[g % NT][:, :, :], src).then_inc(s_t[g % NT], 16)
            def piece(n):
                return x_in[:, n, :].rearrange("p (t h) -> p t h", t=4)

            for q in range(Q):
                n = q % NX
                sp.wait_ge(s_xa, 4 * q + 4)
                sp.dma_start(xa_q[q], piece(n)).then_inc(s_out[n], 16)
                if 1 <= q <= Q - NX:
                    sp.wait_ge(s_stat, 4 * q)
                    m = (q - 1) % NX
                    sp.wait_ge(s_out[m], 16)
                    sp.dma_start(piece(m), x1_q[q - 1 + NX]).then_inc(s_xr[m], 16)
            sp.wait_ge(s_stat, 2 * TILES)
            sp.dma_start(d["moments_a"].rearrange("p (t k) -> p t k", k=2), mom_out[:, :, :]).then_inc(s_mo, 16)
            sp.wait_ge(s_mo, 16)
            for n in range(NX):
                sp.wait_ge(s_out[n], 16 * Q // NX)

        @block.gpsimd
        def _(pool):
            nc.gpsimd.memset(zeros[:, :], 0.0).then_inc(s_pool, 1)
            nc.gpsimd.memset(minus_half[:, :], -0.5).then_inc(s_pst, 1)
            nc.gpsimd.memset(z4[:, :, :, :], 0.0).then_inc(s_pst, 1)
            nc.gpsimd.memset(c4[:, :, :, :], 0.0).then_inc(s_pst, 1)
            pool.wait_ge(s_pst, 1)
            pool.wait_ge(s_dve, 1)
            nc.gpsimd.tensor_tensor(rstd[:, :], small[:, :], minus_half[:, :], ALU.pow).then_inc(s_pst, 1)
            pool.wait_ge(s_dve, 3)
            nc.gpsimd.tensor_tensor(rms[:, :], small[:, :], minus_half[:, :], ALU.pow).then_inc(s_pst, 1)
            for g in range(G):
                pool.wait_ge(s_t[g % NT], 16 * (g // NT) + 16)
                if g >= 2:
                    pool.wait_ge(s_y, g - 1)
                nc.gpsimd.tensor_copy(toep[g % 2][:, :, :], hankel[g % NT][:, :, ::-1]).then_inc(s_flip, 1)

        @block.scalar
        def _(act):
            act.wait_ge(s_in, 192)
            nc.scalar.activation(exp_a[:, :, :], a_nat[:, :, :], ACT.Exp).then_inc(s_act, 1)
            act.wait_ge(s_dve, 5)
            nc.scalar.activation(th[:, :, :], z4[:, :, 0, 0:NST], ACT.Tanh, scale=0.5).then_inc(s_act, 1)
            nc.scalar.activation(z4[:, :, 1:4, 0:NST], z4[:, :, 0, 0:NST].unsqueeze(2).to_broadcast([P, 2, 3, NST]), ACT.Copy).then_inc(s_act, 1)
            act.wait_ge(s_zb, 48)
            nc.scalar.activation(back[:, :, :], back[:, :, :], ACT.Exp, scale=neg_left[:, 0:1]).then_inc(s_back, 1)
            for m in range(4):
                act.wait_ge(s_pwz, m + 1)
                pw = powers[:, m * 16:(m + 1) * 16, :]
                nc.scalar.activation(pw, pw, ACT.Exp, scale=-1.0).then_inc(s_pwe, 1)
            act.wait_ge(s_dve, 11)
            nc.scalar.activation(w128[:, :], z_t[:, :], ACT.Exp, scale=-float(P)).then_inc(s_act, 1)
            for m in range(G // 4):
                act.wait_ge(s_kp, m + 1)
                if m >= 2:
                    act.wait_ge(s_kz[m % 2], 16 * (m // 2))
                nc.scalar.activation(kern[:, m % 2], bank[m % 2][0:4, :].rearrange("p (g t) -> p g t", g=4), ACT.Copy).then_inc(s_ks, 1)
            for m in range(8):
                act.wait_ge(s_sl, m + 1)
                nc.scalar.activation(state[:, 8 * m:8 * m + 8], bank[m][:, :].rearrange("p (g b c) -> p g b c", g=8, b=B), ACT.Copy).then_inc(s_sle, 1)
            for n in range(NX):
                act.dma_start(x_in[:, n, :].rearrange("p (t h) -> p t h", t=4), x1_q[n]).then_inc(s_xr[n], 16)
            with act.Fori(0, G // 16) as h:
                for r in range(2):
                    act.wait_ge(s_y, 16 * h + 8 * r + 8)
                    for i in range(4):
                        uv = u[:, :, G * i:G * i + G].rearrange("p t g -> p g t")
                        nc.scalar.activation(uv[:, bass.ts(2 * h + r, 8), :], bank[4 * r + i][:, :].rearrange("p (g t) -> p g t", g=8), ACT.Copy).then_inc(s_ye, 1)
            act.wait_ge(s_bias, 1)
            with act.Fori(0, Q // NX) as h:
                for n in range(NX):
                    act.wait_ge(s_xr[n], 16 * h + 16)
                    for j in range(4):
                        t = 4 * (NX * h + n) + j
                        xt = x_in[:, n, j * D:(j + 1) * D]
                        nc.scalar.activation(xt, xt, ACT.Identity, bias=bias[:, bass.ds(t, 1)], scale=rstd[:, bass.ds(t, 1)]).then_inc(s_xn, 1)

        @block.vector
        def _(dve):
            dve.wait_ge(s_in, 192)
            nc.vector.tensor_scalar(small[:, :], mom[:, :, 1], LN_EPS, None, ALU.add).then_inc(s_dve, 1)
            dve.wait_ge(s_pst, 4)
            nc.vector.tensor_tensor(small[:, :], rstd[:, :], rstd[:, :], ALU.mult).then_inc(s_dve, 1)
            dve.wait_ge(s_dve, 2)
            nc.vector.tensor_tensor(small[:, :], small[:, :], mom[:, :, 1], ALU.mult).then_inc(s_scan, 1)
            dve.wait_ge(s_scan, 1)
            nc.vector.tensor_scalar(small[:, :], small[:, :], RMS_EPS, None, ALU.add).then_inc(s_dve, 1)
            dve.wait_ge(s_pst, 5)
            nc.vector.tensor_tensor(rms[:, :], rms[:, :], rstd[:, :], ALU.mult).then_inc(s_dve, 1)
            nc.vector.scalar_tensor_tensor(bias[:, :], mom[:, :, 0], -1.0, rstd[:, :], ALU.mult, ALU.mult).then_inc(s_bias, 1)
            dve.wait_ge(s_act, 1)
            nc.vector.tensor_tensor(z4[:, :, 0, 0:NST], exp_a[:, :, :], dt_row[:, :].unsqueeze(1).to_broadcast([P, 2, NST]), ALU.mult).then_inc(s_dve, 1)
            dve.wait_ge(s_act, 2)
            nc.vector.scalar_tensor_tensor(th1[:, :, :], th[:, :, :], 1.0, exp_a[:, :, :], ALU.add, ALU.mult).then_inc(s_dve, 1)
            dve.wait_ge(s_dve, 6)
            nc.vector.reciprocal(th1[:, :, :], th1[:, :, :]).then_inc(s_dve, 1)
            nc.vector.scalar_tensor_tensor(th[:, :, :], th[:, :, :], 2.0, b_nat[:, :, :], ALU.mult, ALU.mult).then_inc(s_dve, 1)
            dve.wait_ge(s_dve, 8)
            nc.vector.tensor_tensor(th[:, :, :], th[:, :, :], th1[:, :, :], ALU.mult).then_inc(s_dve, 1)
            dve.wait_ge(s_dve, 9)
            dve.wait_ge(s_pst, 3)
            for k in range(2):
                src = th[:, k, :].unsqueeze(1).to_broadcast([P, 4, NST])
                ins = nc.vector.scalar_tensor_tensor(c4[:, k, :, 0:NST], src, scale_nat[:, k:k + 1], c_nat[:, k, :].unsqueeze(1).to_broadcast([P, 4, NST]), ALU.mult, ALU.mult)
            ins.then_inc(s_dve, 1)
            dve.wait_ge(s_pe, 1)
            for i in range(4):
                o = (i // 2) * P + (i % 2) * G
                nc.vector.tensor_copy(z_t[32 * i:32 * i + 32, :], bank[0][32 * i:32 * i + 32, o:o + G])
                ins = nc.vector.tensor_copy(c_t[32 * i:32 * i + 32, :], bank[0][32 * i:32 * i + 32, D + o:D + o + G])
            ins.then_inc(s_dve, 1)
            dve.wait_ge(s_dve, 11)
            for m in range(4):
                gs = slice(m * 16, (m + 1) * 16)
                nc.vector.tensor_tensor(powers[:, gs, :], z_t[:, gs].unsqueeze(2).to_broadcast([P, 16, P + 1]),
                                        lags[:, :].unsqueeze(1).to_broadcast([P, 16, P + 1]), ALU.mult).then_inc(s_pwz, 1)
            for m in range(4):
                gs = slice(m * 16, (m + 1) * 16)
                dve.wait_ge(s_pwe, m + 1)
                nc.vector.tensor_tensor(powers[:, gs, :], powers[:, gs, :], c_t[:, gs].unsqueeze(2).to_broadcast([P, 16, P + 1]), ALU.mult).then_inc(s_pw, 1)
            nc.vector.tensor_tensor(d4[:, :], d4[:, :], s4[:, :], ALU.mult).then_inc(s_dve, 1)
            dve.wait_ge(s_dve, 12)
            for m in range(G // 4):
                dve.wait_ge(s_x[4 * m // CH], 16)
                for t in range(4 * m, 4 * m + 4):
                    nc.vector.tensor_scalar(u[:, t, :], u[:, t, :], mom[:, t, 0:1], rms[:, t:t + 1], ALU.subtract, ALU.mult).then_inc(s_u, 1)
                dve.wait_ge(s_ks, m + 1)
                nc.vector.tensor_tensor(kern[:, m % 2, :, P - 1], kern[:, m % 2, :, P - 1], d4[:, 4 * m:4 * m + 4], ALU.add).then_inc(s_kd, 1)
            dve.wait_ge(s_act, 4)
            dve.wait_ge(s_sle, 8)
            wb = w128[:, :].unsqueeze(2).to_broadcast([P, G, B])
            step = 1
            for c in range(1, CH):
                nc.vector.tensor_tensor(carry[:, :, :], state[:, :, :, c - 1], wb, ALU.mult).then_inc(s_scan, 1)
                dve.wait_ge(s_scan, step + 1)
                nc.vector.tensor_tensor(state[:, :, :, c], state[:, :, :, c], carry[:, :, :], ALU.add).then_inc(s_scan, 1)
                dve.wait_ge(s_scan, step + 2)
                step += 2
            dve.wait_ge(s_ye, G // 2)
            with dve.Fori(0, Q // NX) as h:
                for n in range(NX):
                    for j in range(4):
                        t = 4 * (NX * h + n) + j
                        xt = x_in[:, n, j * D:(j + 1) * D]
                        dve.wait_ge(s_xn, t + 1)
                        nc.vector.tensor_tensor(xt, xt, u[:, t, :], ALU.add).then_inc(s_xa, 1)
                    for j in range(4):
                        t = 4 * (NX * h + n) + j
                        dve.wait_ge(s_xa, t + 1)
                        nc.vector.bn_stats(st[:, t, :], x_in[:, n, j * D:(j + 1) * D]).then_inc(s_stat, 1)
            dve.wait_ge(s_stat, TILES)
            for t in range(TILES):
                nc.vector.bn_aggr(mom_out[:, t, :], st[:, t, :]).then_inc(s_stat, 1)

        @block.tensor
        def _(pe):
            pe.wait_ge(s_in, 192)
            pe.wait_ge(s_dve, 10)
            pe.wait_ge(s_act, 3)
            for k in range(2):
                nc.tensor.transpose(bank[0][:, k * P:(k + 1) * P], z4[:, k, :, :].rearrange("p a b -> p (a b)"), ident[:, :])
            for k in range(2):
                ins = nc.tensor.transpose(bank[0][:, D + k * P:D + (k + 1) * P], c4[:, k, :, :].rearrange("p a b -> p (a b)"), ident[:, :])
            ins.then_inc(s_pe, 1)
            pe.wait_ge(s_dve, 11)
            for m in range(G // 4):
                pe.wait_ge(s_pw, m // 4 + 1)
                if m >= 2:
                    pe.wait_ge(s_ks, m - 1)
                nc.tensor.matmul(bank[m % 2][0:4, :], quad_ones[:, :], powers[:, 4 * m:4 * m + 4, P - 1::-1], start=True, stop=True).then_inc(s_kp, 1)
            pe.wait_ge(s_u, TILES)
            pe.wait_ge(s_back, 1)
            pe.wait_ge(s_ks, G // 4)
            for m in range(8):
                for r in range(8):
                    g = 8 * m + r
                    for i in range(4):
                        ins = nc.tensor.matmul(bank[m][32 * i:32 * i + 32, 64 * r:64 * r + 64], back[:, G * i + g, :], u[:, :, G * i + g], start=True, stop=True)
                ins.then_inc(s_sl, 1)
            pe.wait_ge(s_scan, 2 * (CH - 1) + 1)
            pe.wait_ge(s_pw, 4)
            for g in range(G):
                pe.wait_ge(s_flip, g + 1)
                for i in range(4):
                    if g % 8 == 0 and g >= 16:
                        pe.wait_ge(s_ye, 4 * (g // 8 - 2) + i + 1)
                    out = bank[4 * (g // 8 % 2) + i][:, (g % 8) * 64:(g % 8) * 64 + 64]
                    nc.tensor.matmul(out, toep[g % 2][:, i, :], u[:, :, G * i + g], start=True, stop=False)
                    q = slice(32 * i, 32 * i + 32)
                    ins = nc.tensor.matmul(out.rearrange("p (b c) -> p b c", b=B)[:, :, 1:CH], powers[q, g, 1:P + 1], state[q, g, :, 0:CH - 1], start=False, stop=True)
                ins.then_inc(s_y, 1)


def feed_forward(nc, ctx, d, moe):
    EX, DFF = 8, 1024
    FC = DFF // P
    GROUPS = (EX * CAP if moe else N) // 512
    UN = 8 if moe else 2
    PER = 4
    with ExitStack() as mem:
        pre = "moe_" if moe else "mlp_"

        def sb(name, shape, dt=F32):
            return mem.enter_context(nc.sbuf_tensor(pre + name, shape, dt))

        def sem(name):
            return ctx.enter_context(nc.semaphore(pre + name))

        xt_bank = [mem.enter_context(nc.psum_tensor(f"{pre}xt_bank{i}", [P, 512], F32)) for i in range(2)]
        h_bank = [mem.enter_context(nc.psum_tensor(f"{pre}h_bank{i}", [P, 512], F32)) for i in range(4)]
        o_bank = [mem.enter_context(nc.psum_tensor(f"{pre}o_bank{i}", [P, 512], F32)) for i in range(2)]

        NW = 2 if moe else 1
        ident = sb("ident", [P, P])
        w1 = sb("w1", [P, 2, DFF])
        w2 = sb("w2", [P, FC, D])
        w1_h = [sb(f"w1_h{i}", [P, 2, DFF], F22) for i in range(NW)]
        w1_l = [sb(f"w1_l{i}", [P, 2, DFF], F22) for i in range(NW)]
        w2_h = [sb(f"w2_h{i}", [P, FC, D], F22) for i in range(NW)]
        w2_l = [sb(f"w2_l{i}", [P, FC, D], F22) for i in range(NW)]
        NB1 = EX * FC if moe else FC
        b1_rows = sb("b1_rows", [NB1, P])
        b1 = sb("b1", [P, NB1])
        b2 = sb("b2", [P, EX if moe else 1, D])
        xin = [sb(f"xin{i}", [P, 4, D]) for i in range(2)]
        h = [sb(f"h{i}", [P, 4, D]) for i in range(0 if moe else 2)]
        ht_h = [sb(f"ht_h{i}", [P, 2, 512], F22) for i in range(2)]
        ht_l = [sb(f"ht_l{i}", [P, 2, 512], F22) for i in range(2)]
        act_raw = [sb(f"act_raw{i}", [P, 512]) for i in range(4)]
        act_h = [sb(f"act_h{i}", [P, FC, 512], F22) for i in range(2)]
        act_l = [sb(f"act_l{i}", [P, FC, 512], F22) for i in range(2)]
        res = [sb(f"res{i}", [P, 4, D]) for i in range(2)]

        s_in, s_prep, s_b1 = sem("in"), sem("prep"), sem("b1")
        s_w = sem("weights")
        s_x = [sem(f"x{i}") for i in range(2)]
        s_xt, s_hth, s_ht = sem("rows_turned"), sem("ht_high"), sem("ht")
        s_h1, s_a, s_ah, s_al = sem("hidden"), sem("activated"), sem("activated_high"), sem("activated_low")
        s_o, s_free = sem("product"), sem("product_taken")
        s_wh, s_wl = sem("weights_high"), sem("weights_low")
        s_out = [sem(f"stored{i}") for i in range(2)]
        if not moe:
            mom = sb("mom", [P, TILES, 2])
            ms = sb("ms", [P, TILES])
            rms = sb("rms", [P, TILES])
            minus_half = sb("minus_half", [P, TILES])
            scale2 = sb("scale2", [P, 2])
            s_pool, s_ms, s_rms, s_h, s_base = sem("minus_half"), sem("mean_square"), sem("rms"), sem("h"), sem("base")

        src = d["expert_in" if moe else "xa"]
        dst = d["expert_out" if moe else "s1"]
        rows = "(q p t) h -> q p t h" if moe else "(q t p) h -> q p t h"
        src_q, dst_q = src.rearrange(rows, p=P, t=4), dst.rearrange(rows, p=P, t=4)
        W1 = d["L1_ffn_W1"].rearrange("e (k p) f -> e p k f", p=P) if moe else d["L1_attn_w1"].rearrange("(e k p) f -> e p k f", e=1, p=P)
        W2 = d["L1_ffn_W2"].rearrange("e (c p) h -> e p c h", p=P) if moe else d["L1_attn_w2"].rearrange("(e c p) h -> e p c h", e=1, p=P)
        s_passed = sem("passed")
        block = mem.enter_context(nc.Block())
        M = GROUPS // UN

        def all_groups(eng, body):
            with eng.Fori(0, M - 1) as i:
                body(i, False)
            body(M - 1, True)

        @block.sync
        def _(sp):
            ins = ((ident[:, :], d["ident"]),
                   (b1_rows[:, :], d["L1_ffn_b1"].rearrange("e (c p) -> (e c) p", p=P) if moe else d["L1_attn_b1"].rearrange("(c p) -> c p", p=P)))
            for to, frm in ins:
                sp.dma_start(to, frm).then_inc(s_in, 16)
            if moe:
                sp.dma_start(b2[:, :, :], d["L1_ffn_b2"].unsqueeze(0).to_broadcast([P, EX, D])).then_inc(s_in, 16)
            else:
                sp.dma_start(b2[:, 0, :], d["L1_attn_b2"].unsqueeze(0).to_broadcast([P, D])).then_inc(s_in, 16)
                sp.dma_start(mom[:, :, :], d["moments_a"].rearrange("p (t k) -> p t k", k=2)).then_inc(s_in, 16)
                with nc.allow_non_contiguous_dma(reason="256 scales, once"):
                    sp.dma_start(scale2[:, :], d["L1_attn_scale2"].rearrange("(k p) -> p k", p=P)).then_inc(s_in, 16)
            for n in range(2):
                sp.dma_start(xin[n][:, :, :], src_q[n]).then_inc(s_x[n], 16)
            for n in range(2):
                sp.sem_inc(s_out[n], 16)

            def body(i, last):
                for v in range(UN):
                    k, n = i * UN + v, v % 2
                    if not (last and v >= UN - 2):
                        if moe:
                            sp.wait_ge(s_xt, k + 1)
                        else:
                            sp.wait_ge(s_h, k + 1)
                            sp.wait_ge(s_base, k + 1)
                        sp.dma_start(xin[n][:, :, :], src_q[k + 2]).then_inc(s_x[n], 16)
                    sp.wait_ge(s_free, 2 * k + 4)
                    sp.dma_start(dst_q[k], res[n][:, :, :]).then_inc(s_out[n], 16)
                    if moe and not last and v % PER == PER - 1:
                        e = 2 * i + 2 + v // PER
                        sp.wait_ge(s_wl, 2 * e)
                        sp.dma_start(w1[:, :, :], W1[e]).then_inc(s_w, 16)
                        sp.dma_start(w2[:, :, :], W2[e]).then_inc(s_w, 16)

            all_groups(sp, body)
            for n in range(2):
                sp.wait_ge(s_out[n], 16 + 16 * GROUPS // 2)

        @block.gpsimd
        def _(pool):
            if not moe:
                nc.gpsimd.memset(minus_half[:, :], -0.5).then_inc(s_pool, 1)
                pool.wait_ge(s_pool, 1)
                pool.wait_ge(s_ms, 3)
                nc.gpsimd.tensor_tensor(rms[:, :], ms[:, :], minus_half[:, :], ALU.pow).then_inc(s_rms, 1)
                pool.wait_ge(s_in, 80)
                with pool.Fori(0, GROUPS // 2) as i:
                    for n in range(2):
                        pool.wait_ge(s_x[n], 16 * i + 16)
                        pool.wait_ge(s_out[n], 16 * i + 16)
                        for t in range(4):
                            ins = nc.gpsimd.tensor_tensor(res[n][:, t, :], xin[n][:, t, :], b2[:, 0, :], ALU.add)
                        ins.then_inc(s_base, 1)

        @block.scalar
        def _(act):
            for w in range(NW):
                if w:
                    act.wait_ge(s_wl, 2)
                act.dma_start(w1[:, :, :], W1[w]).then_inc(s_w, 16)
                act.dma_start(w2[:, :, :], W2[w]).then_inc(s_w, 16)
            act.wait_ge(s_b1, 2)

            def body(i, last):
                for v in range(UN):
                    k, n = i * UN + v, v % 2
                    for f in range(FC):
                        act.wait_ge(s_al, FC * k + f + 1)
                        wait_apart(act, s_h1, FC * k + f + 1, s_passed)
                        c = (2 * i + v // PER) * FC + f if moe else f
                        nc.scalar.activation(act_raw[f % 4][:, :], h_bank[f % 4][:, :], ACT.Gelu, bias=b1[:, bass.ds(c, 1)]).then_inc(s_a, 1)

            all_groups(act, body)

        @block.vector
        def _(dve):
            dve.sem_inc(s_free, 2)
            dve.sem_inc(s_al, 4)
            dve.wait_ge(s_b1, 1)
            nc.vector.tensor_copy(b1[:, :], h_bank[0][:, 0:NB1]).then_inc(s_b1, 1)
            if not moe:
                dve.wait_ge(s_in, 80)
                nc.vector.tensor_tensor(ms[:, :], mom[:, :, 0], mom[:, :, 0], ALU.mult).then_inc(s_ms, 1)
                dve.wait_ge(s_ms, 1)
                nc.vector.tensor_tensor(ms[:, :], ms[:, :], mom[:, :, 1], ALU.add).then_inc(s_ms, 1)
                dve.wait_ge(s_ms, 2)
                nc.vector.tensor_scalar(ms[:, :], ms[:, :], RMS_EPS, None, ALU.add).then_inc(s_ms, 1)
                dve.wait_ge(s_w, 32)
                for j in range(2):
                    ins = nc.vector.tensor_scalar(w1[:, j, :], w1[:, j, :], scale2[:, j:j + 1], None, ALU.mult)
                ins.then_inc(s_prep, 1)
                dve.wait_ge(s_rms, 1)
                dve.wait_ge(s_prep, 1)

            def split_weights(w, half, high, low, raw, loads):
                dve.wait_ge(s_w, loads)
                high_part(nc, high[w][:, :, :], raw[:, :, :]).then_inc(s_wh, 1)
                dve.wait_ge(s_wh, half + 1)
                low_part(nc, low[w][:, :, :], raw[:, :, :], high[w][:, :, :]).then_inc(s_wl, 1)

            def split_ht(k, n):
                dve.wait_ge(s_xt, k + 1)
                for j in range(2):
                    high_part(nc, ht_h[n][:, j, :], xt_bank[j][:, :]).then_inc(s_hth, 1)
                for j in range(2):
                    dve.wait_ge(s_hth, 2 * k + j + 1)
                    low_part(nc, ht_l[n][:, j, :], xt_bank[j][:, :], ht_h[n][:, j, :]).then_inc(s_ht, 1)

            def split_activated(k, n):
                for f in range(FC + 1):
                    if f < FC:
                        dve.wait_ge(s_a, FC * k + f + 1)
                        high_part(nc, act_h[n][:, f, :], act_raw[f % 4][:, :]).then_inc(s_ah, 1)
                    if f > 0:
                        dve.wait_ge(s_ah, FC * k + f)
                        low_part(nc, act_l[n][:, f - 1, :], act_raw[(f - 1) % 4][:, :], act_h[n][:, f - 1, :]).then_inc(s_al, 1)

            def normalise(k, half, n):
                dve.wait_ge(s_x[n], 16 * half + 16)
                for t in range(4):
                    ins = nc.vector.tensor_scalar(h[n][:, t, :], xin[n][:, t, :], rms[:, bass.ds(4 * k + t, 1)], None, ALU.mult)
                ins.then_inc(s_h, 1)

            def body(i, last):
                for v in range(UN):
                    k, n = i * UN + v, v % 2
                    if not moe and not (last and v == UN - 1):
                        normalise(k + 1, i * UN // 2 + (v + 1) // 2, 1 - n)
                    split_activated(k, n)
                    if not (last and v == UN - 1):
                        split_ht(k + 1, 1 - n)
                    if moe and not (last and v >= PER) and v % PER in (1, 2):
                        e, w = 2 * i + v // PER + 1, 1 - v // PER
                        split_weights(w, 2 * e + v % PER - 1, *(((w1_h, w1_l, w1), (w2_h, w2_l, w2))[v % PER - 1]), 32 * e + 32)
                    if moe:
                        dve.wait_ge(s_out[n], 16 * (i * UN // 2 + v // 2) + 16)
                    else:
                        dve.wait_ge(s_base, k + 1)
                    for o in range(2):
                        dve.wait_ge(s_o, 2 * k + o + 1)
                        to = res[n][:, 2 * o:2 * o + 2, :]
                        base = b2[:, bass.ds(2 * i + v // PER, 1), :].to_broadcast([P, 2, D]) if moe else to
                        nc.vector.tensor_tensor(to, o_bank[o][:, :].rearrange("p (t h) -> p t h", t=2), base, ALU.add).then_inc(s_free, 1)

            if not moe:
                normalise(0, 0, 0)
            else:
                dve.wait_ge(s_in, 48)
            split_ht(0, 0)
            split_weights(0, 0, w1_h, w1_l, w1, 32)
            split_weights(0, 1, w2_h, w2_l, w2, 32)
            all_groups(dve, body)

        @block.tensor
        def _(pe):
            pe.wait_ge(s_in, 48 if moe else 80)
            nc.tensor.transpose(h_bank[0][:, 0:NB1], b1_rows[:, :], ident[0:NB1, 0:NB1]).then_inc(s_b1, 1)
            pe.wait_ge(s_b1, 2)

            def turn(k, half, n):
                if moe:
                    pe.wait_ge(s_x[n], 16 * half + 16)
                    rows = xin[n]
                else:
                    pe.wait_ge(s_h, k + 1)
                    rows = h[n]
                for j in range(2):
                    for t in range(4):
                        ins = nc.tensor.transpose(xt_bank[j][:, t * P:(t + 1) * P], rows[:, t, j * P:(j + 1) * P], ident[:, :])
                ins.then_inc(s_xt, 1)

            def body(i, last):
                for v in range(UN):
                    k, n = i * UN + v, v % 2
                    w = v // PER if moe else 0
                    pe.wait_ge(s_ht, 2 * k + 2)
                    if moe and v % PER == 0:
                        pe.wait_ge(s_wl, 2 * (2 * i + v // PER) + 1)
                    elif not moe and v == 0:
                        pe.wait_ge(s_wl, 1)
                    for f in range(FC):
                        if f >= 4:
                            pe.wait_ge(s_a, FC * k + f - 3)
                        fs = slice(f * P, (f + 1) * P)
                        for j in range(2):
                            out = h_bank[f % 4][:, :]
                            nc.tensor.matmul(out, w1_h[w][:, j, fs], ht_h[n][:, j, :], start=(j == 0), stop=False)
                            nc.tensor.matmul(out, w1_h[w][:, j, fs], ht_l[n][:, j, :], start=False, stop=False)
                            ins = nc.tensor.matmul(out, w1_l[w][:, j, fs], ht_h[n][:, j, :], start=False, stop=(j == 1))
                        ins.then_inc(s_h1, 1)
                    if not (last and v == UN - 1):
                        turn(k + 1, i * UN // 2 + (v + 1) // 2, 1 - n)
                    if moe and v % PER == 0:
                        pe.wait_ge(s_wl, 2 * (2 * i + v // PER) + 2)
                    elif not moe and v == 0:
                        pe.wait_ge(s_wl, 2)
                    for t in range(4):
                        if t % 2 == 0:
                            pe.wait_ge(s_free, 2 * k + t // 2 + 1)
                        ts = slice(t * P, (t + 1) * P)
                        for f in range(FC):
                            if t == 0:
                                pe.wait_ge(s_al, FC * k + f + 5)
                            out = o_bank[t // 2][:, (t % 2) * D:(t % 2 + 1) * D]
                            nc.tensor.matmul(out, act_h[n][:, f, ts], w2_h[w][:, f, :], start=(f == 0), stop=False)
                            nc.tensor.matmul(out, act_h[n][:, f, ts], w2_l[w][:, f, :], start=False, stop=False)
                            ins = nc.tensor.matmul(out, act_l[n][:, f, ts], w2_h[w][:, f, :], start=False, stop=(f == FC - 1))
                        if t % 2 == 1:
                            ins.then_inc(s_o, 1)

            turn(0, 0, 0)
            all_groups(pe, body)


def phase_mlp(nc, ctx, d):
    feed_forward(nc, ctx, d, False)


def phase_moe(nc, ctx, d):
    feed_forward(nc, ctx, d, True)


def phase_qkv(nc, ctx, d):
    with ExitStack() as mem:
        def sb(name, shape, dt=F32):
            return mem.enter_context(nc.sbuf_tensor("qkv_" + name, shape, dt))

        def sem(name):
            return ctx.enter_context(nc.semaphore("qkv_" + name))

        def bank(name):
            return mem.enter_context(nc.psum_tensor("qkv_" + name, [P, 512], F32))

        ht_bank = [bank("ht_bank0"), bank("ht_bank1")]
        qk_bank = [bank("qk_bank0"), bank("qk_bank1")]
        v_bank = [bank("v_bank0"), bank("v_bank1")]
        t_bank = [bank("t_bank0"), bank("t_bank1")]
        ident = sb("ident", [P, P])
        mom = sb("mom", [P, TILES, 2])
        f2 = sb("f2", [P, TILES])
        small = sb("small", [P, TILES])
        minus_half = sb("minus_half", [P, TILES])
        ln_g = sb("ln_g", [P, 2])
        ln_b = sb("ln_b", [P, 2])
        w = sb("w", [P, 2, 3 * D])
        rope_c = sb("rope_c", [P, CH, 2, HD])
        rope_s = sb("rope_s", [P, CH, 2, HD])
        xin = [sb(f"xin{i}", [P, 4, D]) for i in range(2)]
        hn = [sb(f"hn{i}", [P, 4, D]) for i in range(2)]
        ht = sb("ht", [P, 2, 512])
        ht_h = [sb(f"ht_h{i}", [P, 2, 512], F22) for i in range(2)]
        ht_l = [sb(f"ht_l{i}", [P, 2, 512], F22) for i in range(2)]
        w_h = sb("w_h", [P, 2, 3 * D], F22)
        w_l = sb("w_l", [P, 2, 3 * D], F22)
        v_sb = [sb(f"v{i}", [P, 4, D]) for i in range(2)]
        ca = [sb(f"ca{i}", [P, 2, NH, HD]) for i in range(2)]
        sw = [sb(f"sw{i}", [P, 2, NH, HD]) for i in range(2)]
        rot = [sb(f"rot{i}", [P, 4, 512]) for i in range(2)]
        part = [[sb(f"part{j}_{i}", [P, 512], BF16) for j in range(3)] for i in range(4)]
        rest = [sb(f"rest{i}", [P, 512]) for i in range(2)]

        s_in, s_c, s_pool, s_pow = sem("in"), sem("factors"), sem("minus_half"), sem("pow")
        s_x = [sem("x0"), sem("x1")]
        s_hn, s_tt, s_ht = sem("hn"), sem("turned"), sem("ht")
        s_wh, s_hh, s_hl = sem("weights_split"), sem("ht_high"), sem("ht_low")
        s_qk, s_v, s_vk, s_cs, s_rot = sem("qk"), sem("v_ready"), sem("v_kept"), sem("cos_sin"), sem("rotated")
        s_t, s_p0, s_r, s_p1, s_p2 = sem("qk_turned"), sem("part0"), sem("rest"), sem("part1"), sem("part2")
        s_vo = [sem("v_stored0"), sem("v_stored1")]
        s_po = [sem(f"parts_stored{a}") for a in range(4)]
        block = mem.enter_context(nc.Block())
        x_q = d["x1"].rearrange("(q t p) h -> q p t h", p=P, t=4)
        v_q = d["v"].rearrange("(q t p) h -> q p t h", p=P, t=4)
        Q = TILES // 4

        def groups(eng, group):
            for n in range(2):
                group(n, n, n == 0, False)
            with eng.Fori(1, Q // 2 - 1) as i:
                for n in range(2):
                    group(2 * i + n, n, False, False)
            for n in range(2):
                group(Q - 2 + n, n, False, False)
            group(Q, 0, False, True)

        def is_group(k, n):
            return isinstance(k, int) and k == n

        @block.sync
        def _(sp):
            for to, frm in ((ident[:, :], d["ident"]), (mom[:, :, :], d["moments1"].rearrange("p (t k) -> p t k", k=2)),
                            (rope_c[:, :, :, :].rearrange("p a b c -> p (a b c)"), d["rope_c"]), (rope_s[:, :, :, :].rearrange("p a b c -> p (a b c)"), d["rope_s"])):
                sp.dma_start(to, frm).then_inc(s_in, 16)
            sp.dma_start(xin[0][:, :, :], x_q[0]).then_inc(s_x[0], 16)
            sp.dma_start(w[:, :, :], d["L1_ffn_Wqkv"].rearrange("(k p) c -> p k c", p=P)).then_inc(s_in, 16)
            sp.dma_start(xin[1][:, :, :], x_q[1]).then_inc(s_x[1], 16)
            with nc.allow_non_contiguous_dma(reason="256 scales and shifts, once"):
                sp.dma_start(ln_g[:, :], d["L1_ffn_ln1_g"].rearrange("(k p) -> p k", p=P)).then_inc(s_in, 16)
                sp.dma_start(ln_b[:, :], d["L1_ffn_ln1_b"].rearrange("(k p) -> p k", p=P)).then_inc(s_in, 16)

            def store_v(k, n):
                sp.wait_ge(s_vk, 4 * k + 4)
                sp.dma_start(v_q[k], v_sb[n][:, :, :]).then_inc(s_vo[n], 16)

            def store_parts(k):
                for a in range(4):
                    sp.wait_ge(s_p2, 4 * k + a + 1)
                    for j in range(3):
                        sp.dma_start(d["parts"][3 * (a // 2) + j, (a % 2) * P:(a % 2 + 1) * P, bass.ts(k, 512)], part[a][j][:, :]).then_inc(s_po[a], 16)

            def group(k, n, first, last):
                if not last:
                    sp.wait_ge(s_hn, k + 1)
                    sp.dma_start(xin[n][:, :, :], x_q[k + 2]).then_inc(s_x[n], 16)
                if not first:
                    store_parts(k - 1)
                store_v(k, n)

            for n in range(2):
                group(n, n, n == 0, False)
            with sp.Fori(1, Q // 2 - 1) as i:
                for n in range(2):
                    group(2 * i + n, n, False, False)
            for n in range(2):
                group(Q - 2 + n, n, False, True)
            store_parts(Q - 1)
            for n in range(2):
                sp.wait_ge(s_vo[n], 16 * Q // 2)
            for a in range(4):
                sp.wait_ge(s_po[a], 48 * Q)

        @block.gpsimd
        def _(pool):
            nc.gpsimd.memset(minus_half[:, :], -0.5).then_inc(s_pool, 1)
            pool.wait_ge(s_pool, 1)
            pool.wait_ge(s_c, 2)
            nc.gpsimd.tensor_tensor(f2[:, :], small[:, :], minus_half[:, :], ALU.pow).then_inc(s_pow, 1)

            def group(k, n, first, last):
                for t in range(4):
                    if not last:
                        e = 4 * k + t
                        need(pool, s_cs, 3 * e + 3)
                        if t == 0:
                            need(pool, s_t, 4 * k - 4)
                        nc.gpsimd.tensor_tensor(rot[n][:, t, :], ca[t % 2][:, :, :, :].rearrange("p a b c -> p (a b c)"),
                                                sw[t % 2][:, :, :, :].rearrange("p a b c -> p (a b c)"), ALU.add).then_inc(s_rot, 1)
                    if not first:
                        pool.wait_ge(s_p1, 4 * (k - 1) + t + 1)
                        nc.gpsimd.tensor_tensor(part[t][2][:, :], rest[t % 2][:, :], part[t][1][:, :], ALU.subtract).then_inc(s_p2, 1)

            groups(pool, group)

        @block.scalar
        def _(act):
            act.wait_ge(s_in, 112)

            def take_ht(k, n):
                act.wait_ge(s_tt, k + 1)
                need(act, s_hl, 2 * k)
                for j in range(2):
                    ins = nc.scalar.activation(ht[:, j, :], ht_bank[j][:, :], ACT.Identity, bias=ln_b[:, j:j + 1], scale=ln_g[:, j:j + 1])
                ins.then_inc(s_ht, 1)

            def group(k, n, first, last):
                for t in range(4):
                    if not first:
                        e = 4 * (k - 1) + t
                        act.wait_ge(s_t, e + 1)
                        need(act, s_po[t], 48 * (k - 1))
                        nc.scalar.activation(part[t][0][:, :], t_bank[t % 2][:, :], ACT.Identity).then_inc(s_p0, 1)
                    if not last:
                        act.wait_ge(s_v, 4 * k + t + 1)
                        if t == 0:
                            need(act, s_vo[n], 8 * k - 8 * n)
                        nc.scalar.activation(v_sb[n][:, t, :], v_bank[t % 2][:, 0:D], ACT.Identity).then_inc(s_vk, 1)
                    if not first:
                        act.wait_ge(s_r, e + 1)
                        nc.scalar.activation(part[t][1][:, :], rest[t % 2][:, :], ACT.Identity).then_inc(s_p1, 1)
                    if t == 0 and not last and not is_group(k, Q - 1):
                        take_ht(k + 1, 1 - n)

            take_ht(0, 0)
            groups(act, group)

        @block.vector
        def _(dve):
            dve.wait_ge(s_in, 112)
            nc.vector.tensor_scalar(small[:, :], mom[:, :, 1], LN_EPS, LN_EPS, ALU.add, ALU.mult).then_inc(s_c, 1)
            dve.wait_ge(s_c, 1)
            nc.vector.tensor_tensor(small[:, :], small[:, :], mom[:, :, 1], ALU.add).then_inc(s_c, 1)
            dve.wait_ge(s_pow, 1)

            def normalise(k, n):
                dve.wait_ge(s_x[n], 8 * k - 8 * n + 16)
                for t in range(4):
                    ins = nc.vector.tensor_scalar(hn[n][:, t, :], xin[n][:, t, :], mom[:, 4 * k + t, 0:1], f2[:, bass.ds(4 * k + t, 1)], ALU.subtract, ALU.mult)
                ins.then_inc(s_hn, 1)

            def rope(k, n, t):
                e = 4 * k + t
                dve.wait_ge(s_qk, e + 1)
                need(dve, s_rot, e - 1)
                qk = qk_bank[t % 2][:, :].rearrange("p (a h c) -> p a h c", a=2, c=HD)
                c = 4 * n + t
                H2 = HD // 2

                def table(tab, lo, hi):
                    return tab[:, c, :, lo:hi].unsqueeze(2).to_broadcast([P, 2, NH, hi - lo])

                nc.vector.tensor_tensor(ca[t % 2][:, :, :, :], qk, table(rope_c, 0, HD), ALU.mult).then_inc(s_cs, 1)
                nc.vector.tensor_tensor(sw[t % 2][:, :, :, 0:H2], qk[:, :, :, H2:HD], table(rope_s, 0, H2), ALU.mult).then_inc(s_cs, 1)
                nc.vector.tensor_tensor(sw[t % 2][:, :, :, H2:HD], qk[:, :, :, 0:H2], table(rope_s, H2, HD), ALU.mult).then_inc(s_cs, 1)

            def group(k, n, first, last):
                if not last and not is_group(k, Q - 1):
                    normalise(k + 1, 1 - n)
                for t in range(4):
                    if not last:
                        rope(k, n, t)
                    if not first:
                        e = 4 * (k - 1) + t
                        dve.wait_ge(s_p0, e + 1)
                        need(dve, s_p2, e - 1)
                        nc.vector.tensor_tensor(rest[t % 2][:, :], t_bank[t % 2][:, :], part[t][0][:, :], ALU.subtract).then_inc(s_r, 1)
                    if t == 1 and not last and not is_group(k, Q - 1):
                        split_ht(k + 1, 1 - n)

            def split_ht(k, n):
                dve.wait_ge(s_ht, k + 1)
                for j in range(2):
                    high_part(nc, ht_h[n][:, j, :], ht[:, j, :]).then_inc(s_hh, 1)
                for j in range(2):
                    dve.wait_ge(s_hh, 2 * k + j + 1)
                    low_part(nc, ht_l[n][:, j, :], ht[:, j, :], ht_h[n][:, j, :]).then_inc(s_hl, 1)

            normalise(0, 0)
            high_part(nc, w_h[:, :, :], w[:, :, :]).then_inc(s_wh, 1)
            dve.wait_ge(s_wh, 1)
            low_part(nc, w_l[:, :, :], w[:, :, :], w_h[:, :, :]).then_inc(s_wh, 1)
            split_ht(0, 0)
            groups(dve, group)

        @block.tensor
        def _(pe):
            pe.wait_ge(s_in, 112)

            def turn(k, n):
                pe.wait_ge(s_hn, k + 1)
                for j in range(2):
                    for t in range(4):
                        ins = nc.tensor.transpose(ht_bank[j][:, t * P:(t + 1) * P], hn[n][:, t, j * P:(j + 1) * P], ident[:, :])
                ins.then_inc(s_tt, 1)

            pe.wait_ge(s_wh, 2)
            w_part = [[x[:, j, :].rearrange("p (h a c) -> p a h c", a=3, c=HD) for j in range(2)] for x in (w_h, w_l)]

            def group(k, n, first, last):
                if not last:
                    pe.wait_ge(s_hl, 2 * k + 2)
                for t in range(4):
                    e = 4 * k + t
                    if not last:
                        need(pe, s_cs, 3 * e - 3)
                        need(pe, s_vk, e - 1)
                        ts = slice(t * P, (t + 1) * P)
                        for out, cols, ready in ((qk_bank[t % 2][:, :], slice(0, 2), s_qk), (v_bank[t % 2][:, 0:D], 2, s_v)):
                            for j in range(2):
                                nc.tensor.matmul(out, ht_h[n][:, j, ts], w_part[0][j][:, cols], start=(j == 0), stop=False)
                                nc.tensor.matmul(out, ht_h[n][:, j, ts], w_part[1][j][:, cols], start=False, stop=False)
                                ins = nc.tensor.matmul(out, ht_l[n][:, j, ts], w_part[0][j][:, cols], start=False, stop=(j == 1))
                            ins.then_inc(ready, 1)
                    if not first:
                        if t == 0:
                            pe.wait_ge(s_rot, 4 * k)
                        need(pe, s_r, e - 4 - 1)
                        for u in range(4):
                            ins = nc.tensor.transpose(t_bank[t % 2][:, u * P:(u + 1) * P], rot[1 - n][:, u, t * P:(t + 1) * P], ident[:, :])
                        ins.then_inc(s_t, 1)
                    if t == 0 and not last and not is_group(k, Q - 1):
                        turn(k + 1, 1 - n)

            turn(0, 0)
            groups(pe, group)


MAX_PIECES = [(qt, j, 2) for qt in range(4) for j in (0, 2)] + [(qt, j, 1) for qt in range(4, CH) for j in range(4)]
HALF_DONE = (7, 23)


def attention_order():
    steps = [(h, kt) for h in range(2) for kt in range(4 * h + 4)]
    width = [min(4 * (h + 1) - kt, 4) * P for h, kt in steps]
    main = []
    for s in range(len(steps)):
        ahead = s + 1
        main += [("st", ahead, j, (width[ahead] if ahead < len(steps) else width[0]) + 260) for j in range(4)]
        main.append(("pv", s, None, 0))
        if s == 1:
            main.append(("ring", ("out", 1), None, 0))
        if s == 6:
            main.append(("ring", ("out", 0), None, 0))
    side = []
    for n, (qt, _, heads) in enumerate(MAX_PIECES):
        side.append(("ring", ("max", n), None, heads * (qt + 1) * P + 260))
        if n == 2:
            side.append(("ring", ("row", 1), None, 0))
        if n == 10:
            side.append(("ring", ("row", 0), None, 0))
    total_m, total_s = sum(x[3] for x in main), sum(x[3] for x in side)
    order, dm, ds, im, is_ = [], 0, 0, 0, 0
    while im < len(main) or is_ < len(side):
        if is_ == len(side) or (im < len(main) and dm * total_s <= ds * total_m):
            order.append(main[im][:3])
            dm += main[im][3]
            im += 1
        else:
            order.append(side[is_][:3])
            ds += side[is_][3]
            is_ += 1
    return steps, order


def phase_attention(nc, ctx, d):
    UNITS = B * NH // 4
    KR = 6 * HD
    STEPS, ORDER = attention_order()
    NS = len(STEPS)
    RING = len(MAX_PIECES) + 4
    with ExitStack() as mem:
        def sb(name, shape, dt=F32):
            return mem.enter_context(nc.sbuf_tensor("at_" + name, shape, dt))

        def sem(name):
            return ctx.enter_context(nc.semaphore("at_" + name))

        ring = [mem.enter_context(nc.psum_tensor(f"at_ring{i}", [P, 2 * 512], F32)) for i in range(2)]
        st_bank = [mem.enter_context(nc.psum_tensor(f"at_st{i}", [P, 512], F32)) for i in range(3)]
        pv_bank = mem.enter_context(nc.psum_tensor("at_pv", [P, 512], F32))

        ident = sb("ident", [P, P])
        ident_b = sb("ident_b", [P, P], BF16)
        mask_t = sb("mask_t", [P, P], BF16)
        masks_in = sb("masks_in", [P, 2 * P])
        mask_q = sb("mask_q", [P, P], BF16)
        q_s = [sb(f"q{i}", [KR + 3, 4, L], BF16) for i in range(4)]
        k_s = [sb(f"k{i}", [KR + 3, 4, L], BF16) for i in range(4)]
        v_in = [sb(f"v_in{i}", [P, CH, 4 * HD]) for i in range(2)]
        v_a = [sb(f"v_a{i}", [P, CH, 4, 32]) for i in range(4)]
        top = [sb(f"top{i}", [P, 4, 4]) for i in range(2)]
        top_rest = sb("top_rest", [P, 2, 4, 4])
        top_p = [sb(f"top_p{i}", [P, 4, 12], BF16)    for i in range(2)]
        top_row = [sb(f"top_row{i}", [12, 512], BF16) for i in range(2)]
        prob = [sb(f"prob{i}", [P, 512]) for i in range(8)]
        pv_sb = [sb(f"pv_sb{i}", [P, 512]) for i in range(2)]
        inv = sb("inv", [P, 2, 4, 4])
        zeros = sb("zeros", [P, 4 * D])
        o_sb = [sb(f"o{i}", [P, 4, 4 * HD]) for i in range(2)]

        s_in, s_ones, s_kones, s_b16 = sem("in"), sem("value_ones"), sem("key_ones"), sem("bfloat16_tables")
        s_qk = [sem(f"qk_loaded{i}") for i in range(4)]
        s_vl = [sem("v_loaded0"), sem("v_loaded1")]
        s_va = sem("v_spread")
        s_ring, s_read = sem("ring_written"), sem("ring_read")
        s_sp, s_split = sem("split_step"), sem("split")
        s_row = [sem("rows_placed0"), sem("rows_placed1")]
        s_st, s_exp, s_pv, s_ev = sem("turned_scores"), sem("exponentials"), sem("weighted_values"), sem("values_kept")
        s_passed, s_passed_pool = sem("passed"), sem("passed_pool")
        s_inv, s_zeros, s_zeroed = sem("inverse"), sem("zeros"), sem("expert_in_zeroed")
        s_os = [sem("output_stored0"), sem("output_stored1")]
        block = mem.enter_context(nc.Block())

        RING_ITEMS = [item for kind, item, _ in ORDER if kind == "ring"]
        FIRST_ITEMS = [("max", n) for n in range(10)] + [("row", 0)] + [("max", n) for n in range(10, len(MAX_PIECES))]

        def in_turn(k, item):
            if isinstance(k, int) and k == 0 and item == ("out", 1):
                return False
            return not (isinstance(k, int) and k == UNITS - 1 and (item[0] == "max" or item == ("row", 0)))

        def ring_number(k, item):
            base = len(FIRST_ITEMS) if isinstance(k, int) and k == 0 else RING * k + RING - 4
            return base + [x for x in RING_ITEMS if in_turn(k, x)].index(item)

        def ring_buffer(k, item):
            first = isinstance(k, int) and k == 0
            return ring[(ring_number(0 if first else UNITS - 1 if isinstance(k, int) and k == UNITS - 1 else 1, item)) % 2]

        def turns(eng, turn):
            for v in range(4):
                turn(v, 0, v)
            with eng.Fori(1, B - 1) as b:
                for v in range(4):
                    turn(4 * b + v, b, v)
            for v in range(4):
                turn(UNITS - 4 + v, B - 1, v)

        def is_unit(k, n):
            return isinstance(k, int) and k == n

        @block.sync
        def _(sp):
            for to, frm in ((ident[:, :], d["ident"]), (masks_in[:, :], d["masks"])):
                sp.dma_start(to, frm).then_inc(s_in, 16)
            parts_h = d["parts"].rearrange("j (g h c) n -> j g c h n", h=4, c=HD)
            v_rows = d["v"].rearrange("(b t p) (g c) -> b g p t c", p=P, t=CH, c=4 * HD)
            out_rows = d["attn"].rearrange("(b s t p) (g c) -> b s g p t c", s=2, t=4, p=P, c=4 * HD)

            slot_rows = d["expert_in"].rearrange("(k p r) h -> k p (r h)", k=UNITS, p=P)
            sp.wait_ge(s_zeros, 1)

            def load(b, v, n):
                for i, (jq, jk) in enumerate(((0, 4), (0, 3), (1, 4), (0, 5), (1, 3), (2, 3))):
                    sp.dma_start(q_s[v][16 * i:16 * i + 16, :, :], parts_h[jq, v, :, :, bass.ts(b, L)]).then_inc(s_qk[v], 16)
                    sp.dma_start(k_s[v][16 * i:16 * i + 16, :, :], parts_h[jk, v, :, :, bass.ts(b, L)]).then_inc(s_qk[v], 16)
                sp.dma_start(v_in[n][:, :, :], v_rows[b, v]).then_inc(s_vl[n], 16)

            def place_rows(k, v, half, read):
                wait_apart(sp, s_read, read, s_passed)
                sp.dma_start(q_s[v][KR:KR + 3, :, half * 512:half * 512 + 512], top_row[half][:, :]).then_inc(s_row[half], 16)

            def store(b, v, half, read):
                wait_apart(sp, s_read, read, s_passed)
                sp.dma_start(out_rows[b, half, v], o_sb[half][:, :, :]).then_inc(s_os[half], 16)

            for v in range(3):
                load(0, v, v % 2) if v < 2 else None
            sp.wait_ge(s_va, 1)
            load(0, 2, 0)
            place_rows(0, 0, 0, FIRST_ITEMS.index(("row", 0)) + 1)

            def turn(k, b, v):
                place_rows(k, v, 1, ring_number(k, ("row", 1)) + 1)
                if not (isinstance(k, int) and k + 3 >= UNITS):
                    if not is_unit(k, 0):
                        wait_apart(sp, s_pv, NS * k, s_passed)
                    wait_apart(sp, s_va, k + 2, s_passed)
                    load(b + (1 if v else 0), (v + 3) % 4, (v + 3) % 2)
                if not is_unit(k, 0):
                    store(b - 1 if v == 0 else b, (v - 1) % 4, 1, ring_number(k, ("out", 1)) + 1)
                sp.dma_start(slot_rows[k], zeros[:, :]).then_inc(s_zeroed, 16)
                store(b, v, 0, ring_number(k, ("out", 0)) + 1)
                if not is_unit(k, UNITS - 1):
                    place_rows(k + 1, (v + 1) % 4, 0, ring_number(k, ("row", 0)) + 1)

            turns(sp, turn)
            store(B - 1, 3, 1, RING * (UNITS - 1) + RING - 4 + 3 + 1)
            for half in range(2):
                sp.wait_ge(s_os[half], 16 * UNITS)
            sp.wait_ge(s_zeroed, 16 * UNITS)

        @block.gpsimd
        def _(pool):
            for i in range(4):
                nc.gpsimd.memset(v_a[i][:, :, :, HD:], 1.0).then_inc(s_ones, 1)

            def spread(u, half_u, n, v):
                wait_apart(pool, s_vl[n], 16 * half_u + 16, s_passed_pool)
                nc.gpsimd.tensor_copy(v_a[v][:, :, :, 0:HD], v_in[n][:, :, :].rearrange("p t (h c) -> p t h c", c=HD)).then_inc(s_va, 1)

            pool.wait_ge(s_ones, 4)
            for u in range(3):
                spread(u, u // 2, u % 2, u)

            def turn(k, b, v):
                if not (isinstance(k, int) and k + 3 >= UNITS):
                    need(pool, s_pv, NS * k)
                    spread(k + 3, 2 * b + (v + 3) // 2, (v + 3) % 2, (v + 3) % 4)

            turns(pool, turn)

        @block.scalar
        def _(act):
            def keep(k, half):
                act.wait_ge(s_pv, NS * k + (4 if half == 0 else 12))
                nc.scalar.activation(pv_sb[half][:, :], pv_bank[:, :], ACT.Copy).then_inc(s_ev, 1)

            def turn(k, b, v):
                for s, (half, kt) in enumerate(STEPS):
                    c0 = max(kt - 4 * half, 0) * P
                    for j in range(4):
                        act.wait_ge(s_st, 4 * NS * k + 4 * s + j + 1)
                        if j == 0 and not (is_unit(k, 0) and s < 2):
                            act.wait_ge(s_pv, NS * k + s - 1)
                        nc.scalar.activation(prob[(s % 2) * 4 + j][:, c0:], st_bank[(4 * s + j) % 3][:, c0:], ACT.Exp).then_inc(s_exp, 1)
                    if s == 0 and not is_unit(k, 0):
                        keep(k - 1, 1)
                    if s == 4:
                        keep(k, 0)

            turns(act, turn)
            keep(UNITS - 1, 1)

        @block.vector
        def _(dve):
            nc.vector.memset(zeros[:, :], 0.0).then_inc(s_zeros, 1)
            dve.wait_ge(s_in, 32)
            for to, frm in ((ident_b, ident[:, :]), (mask_q, masks_in[:, 0:P]), (mask_t, masks_in[:, P:])):
                nc.vector.tensor_copy(to[:, :], frm).then_inc(s_b16, 1)
            for i in range(4):
                nc.vector.memset(k_s[i][KR:KR + 3, :, :], 1.0).then_inc(s_kones, 1)

            def ring_item(u, item, number, tile):
                dve.wait_ge(s_ring, number + 1)
                kind, n = item
                if kind == "max":
                    qt, j, heads = MAX_PIECES[n]
                    half = qt // 4
                    if n in (0, HALF_DONE[0] + 1) and not is_unit(u, 0):
                        dve.wait_ge(s_split, 2 * u + half - 1)
                    rows = tile[:, :].rearrange("p (h c) -> p h c", h=heads)[:, :, 0:(qt + 1) * P]
                    nc.vector.tensor_reduce(top[half][:, qt % 4, j:j + heads], rows, AX_X, ALU.max).then_inc(s_read, 1)
                    if n in HALF_DONE:
                        dve.wait_ge(s_read, number + 1)
                        e = 6 * u + 3 * half
                        nc.vector.tensor_scalar(top_p[half][:, :, 0:4], top[half][:, :, :], -1.0, None, ALU.mult).then_inc(s_sp, 1)
                        dve.wait_ge(s_sp, e + 1)
                        nc.vector.scalar_tensor_tensor(top_rest[:, half, :, :], top[half][:, :, :], -1.0, top_p[half][:, :, 0:4], ALU.mult, ALU.subtract).then_inc(s_sp, 1)
                        dve.wait_ge(s_sp, e + 2)
                        nc.vector.tensor_copy(top_p[half][:, :, 4:8], top_rest[:, half, :, :]).then_inc(s_sp, 1)
                        dve.wait_ge(s_sp, e + 3)
                        nc.vector.tensor_tensor(top_p[half][:, :, 8:12], top_rest[:, half, :, :], top_p[half][:, :, 4:8], ALU.subtract).then_inc(s_split, 1)
                elif kind == "row":
                    need(dve, s_row[n], 16 * u)
                    nc.vector.tensor_copy(top_row[n][:, :], tile[0:12, 0:512]).then_inc(s_read, 1)
                else:
                    need(dve, s_os[n], 16 * u)
                    t = tile[:, 0:512].rearrange("p (t h c) -> p t h c", t=4, c=32)
                    nc.vector.reciprocal(inv[:, n, :, :], t[:, :, :, HD]).then_inc(s_inv, 1)
                    dve.wait_ge(s_inv, 2 * u + n + 1)
                    nc.vector.tensor_tensor(o_sb[n][:, :, :].rearrange("p t (h c) -> p t h c", c=HD), t[:, :, :, 0:HD],
                                            inv[:, n, :, :].unsqueeze(3).to_broadcast([P, 4, 4, HD]), ALU.mult).then_inc(s_read, 1)

            for i, item in enumerate(FIRST_ITEMS):
                ring_item(0, item, i, ring[i % 2])

            def turn(k, b, v):
                for item in RING_ITEMS:
                    if in_turn(k, item):
                        u = k if item in (("row", 1), ("out", 0)) else k - 1 if item == ("out", 1) else k + 1
                        ring_item(u, item, ring_number(k, item), ring_buffer(k, item))

            turns(dve, turn)
            ring_item(UNITS - 1, ("out", 1), RING * (UNITS - 1) + RING - 4 + 3, ring[1])

        @block.tensor
        def _(pe):
            pe.wait_ge(s_b16, 3)
            pe.wait_ge(s_ones, 4)
            pe.wait_ge(s_kones, 4)

            def ring_item(u, b, v, item, number, tile):
                need(pe, s_read, number - 1)
                kind, n = item
                if kind == "max":
                    qt, j, heads = MAX_PIECES[n]
                    if n == 0:
                        pe.wait_ge(s_qk[v], 192 * b + 192)
                    width = (qt + 1) * P
                    for h in range(heads):
                        query = q_s[v][0:KR, j + h, qt * P:width]
                        for lo in range(0, width, 512):
                            hi = min(lo + 512, width)
                            nc.tensor.matmul(tile[:, 512 * h + lo:512 * h + hi], query, k_s[v][0:KR, j + h, lo:hi], start=True, stop=hi < width)
                        ins = nc.tensor.matmul(tile[:, 512 * h + qt * P:512 * h + width], ident_b[:, :], mask_q[:, :], start=False, stop=True)
                elif kind == "row":
                    pe.wait_ge(s_split, 2 * u + n + 1)
                    for t in range(4):
                        ins = nc.tensor.matmul(tile[0:12, t * P:(t + 1) * P], top_p[n][:, t, :], ident_b[:, :], start=True, stop=True)
                else:
                    pe.wait_ge(s_ev, 2 * u + n + 1)
                    for t in range(4):
                        ins = nc.tensor.transpose(tile[:, t * P:(t + 1) * P], pv_sb[n][:, t * P:(t + 1) * P], ident[:, :])
                ins.then_inc(s_ring, 1)

            def scores(u, v, s, j):
                half, kt = STEPS[s]
                c0 = max(kt - 4 * half, 0) * P
                if kt == 0 and j == 0:
                    pe.wait_ge(s_row[half], 16 * u + 16)
                if not (is_unit(u, 0) and s == 0 and j < 3):
                    pe.wait_ge(s_exp, 4 * NS * u + 4 * s + j - 2)
                bank = st_bank[(4 * s + j) % 3]
                on_edge = kt >= 4 * half
                ins = nc.tensor.matmul(bank[:, c0:], k_s[v][:, j, kt * P:(kt + 1) * P], q_s[v][:, j, half * 512 + c0:half * 512 + 512],
                                       start=True, stop=not on_edge)
                if on_edge:
                    ins = nc.tensor.matmul(bank[:, c0:c0 + P], ident_b[:, :], mask_t[:, :], start=False, stop=True)
                ins.then_inc(s_st, 1)

            def values(k, v, s):
                half, kt = STEPS[s]
                c0 = max(kt - 4 * half, 0) * P
                pe.wait_ge(s_exp, 4 * NS * k + 4 * s + 4)
                if s == 0:
                    pe.wait_ge(s_va, k + 1)
                if kt == 0:
                    need(pe, s_ev, 2 * k + half)
                for j in range(4):
                    ins = nc.tensor.matmul(pv_bank[32 * j:32 * j + 32, c0:], v_a[v][:, kt, j, :], prob[(s % 2) * 4 + j][:, c0:],
                                           start=(kt == 0), stop=(kt == 4 * half + 3), tile_position=(0, 32 * j))
                ins.then_inc(s_pv, 1)

            for i, item in enumerate(FIRST_ITEMS):
                ring_item(0, 0, 0, item, i, ring[i % 2])
            for j in range(4):
                scores(0, 0, 0, j)

            def turn(k, b, v):
                nxt = (k + 1, b + (1 if v == 3 else 0), (v + 1) % 4)
                for kind, s, j in ORDER:
                    if kind == "st" and s < NS:
                        scores(k, v, s, j)
                    elif kind == "st" and not is_unit(k, UNITS - 1):
                        scores(k + 1, (v + 1) % 4, 0, j)
                    elif kind == "pv":
                        values(k, v, s)
                    elif kind == "ring" and in_turn(k, s):
                        unit = (k, b, v) if s in (("row", 1), ("out", 0)) else (k - 1, b, v) if s == ("out", 1) else nxt
                        ring_item(*unit, s, ring_number(k, s), ring_buffer(k, s))

            turns(pe, turn)
            ring_item(UNITS - 1, B - 1, 3, ("out", 1), RING * (UNITS - 1) + RING - 4 + 3, ring[1])


def phase_gate(nc, ctx, d):
    Q = TILES // 4
    E = EXPERTS
    RS, SS = 9, 10
    with ExitStack() as mem:
        def sb(name, shape, dt=F32):
            return mem.enter_context(nc.sbuf_tensor("gt_" + name, shape, dt))

        def sem(name):
            return ctx.enter_context(nc.semaphore("gt_" + name))

        def bank(name):
            return mem.enter_context(nc.psum_tensor("gt_" + name, [P, 512], F32))

        at_bank = [bank("at_bank0"), bank("at_bank1")]
        pr_bank = [bank("pr_bank0"), bank("pr_bank1")]
        ht_bank = [bank("ht_bank0"), bank("ht_bank1")]
        lg_bank, place_bank = bank("lg_bank"), bank("place_bank")

        ident = sb("ident", [P, P])
        tri = sb("tri", [P, P])
        ones = sb("ones", [P, P])
        lower = sb("lower", [P, E, E])
        slot_base = sb("slot_base", [P, E])
        w_proj = sb("w_proj", [P, 2, D])
        w_gate = sb("w_gate", [P, 2, E])
        g_row = sb("g_row", [P, D])
        b_row = sb("b_row", [P, D])
        mom = sb("mom", [P, TILES, 2])
        small = sb("small", [P, TILES])
        minus_half = sb("minus_half", [P, TILES])
        rstd1 = sb("rstd1", [P, TILES])
        bias1 = sb("bias1", [P, TILES])
        attn_in = [sb(f"attn_in{i}", [P, 4, D]) for i in range(2)]
        x1_in = [sb(f"x1_in{i}", [P, 4, D]) for i in range(2)]
        attn_t = [sb(f"attn_t{i}", [P, 2, 512]) for i in range(2)]
        xn = [sb(f"xn{i}", [P, 4, D]) for i in range(2)]
        x2 = [sb(f"x2_{i}", [P, 4, D]) for i in range(2)]
        stats = sb("stats", [P, 4, 6])
        mv = [sb(f"mv{i}", [P, 4, 2]) for i in range(2)]
        var = [sb(f"var{i}", [P, 4]) for i in range(2)]
        rstd2 = [sb(f"rstd2_{i}", [P, 4]) for i in range(2)]
        bias2 = [sb(f"bias2_{i}", [P, 4]) for i in range(2)]
        hn = [sb(f"hn{i}", [P, 4, D]) for i in range(2)]
        h2 = [sb(f"h2_{i}", [P, 4, D]) for i in range(4)]
        h2_t = [sb(f"h2_t{i}", [P, 2, 512]) for i in range(2)]
        high = sb("high", [P, 4])
        lowered = sb("lowered", [P, 4, E])
        expd = sb("expd", [P, 4, E])
        total = sb("total", [P, 4])
        gates = [sb(f"gates{i}", [P, 4, E]) for i in range(2)]
        above = sb("above", [P, 4, E, E])
        equal = sb("equal", [P, 4, E, E])
        rank = [sb(f"rank{i}", [P, 4, E]) for i in range(2)]
        chosen = [sb(f"chosen{i}", [P, 4, E]) for i in range(2)]
        chosen_sum = sb("chosen_sum", [P, E])
        before = [sb(f"before{i}", [P, E]) for i in range(2)]
        over = sb("over", [P, 4, E])
        slot = sb("slot", [P, 4, E])
        kept = sb("kept", [P, 4, E])
        sel = sb("sel", [P, 2, 4 * E])
        picked = sb("picked", [P, 2, 4 * E])
        picked_w = sb("picked_w", [P, 2, 4 * E])
        slot_f = sb("slot_f", [P, 8])
        idx = [sb(f"idx{i}", [P, 8], I32) for i in range(4)]
        slots_all = sb("slots_all", [P, Q, 8], I32)
        weights_all = sb("weights_all", [P, Q, 8])

        s_in, s_half, s_pre, s_rs1 = sem("in"), sem("minus_half"), sem("pre"), sem("rstd1")
        s_a = [sem("attn0"), sem("attn1")]
        s_x1 = [sem("x1_0"), sem("x1_1")]
        s_at, s_atk, s_pr, s_xn, s_x2 = sem("attn_turned"), sem("attn_t"), sem("projected"), sem("xn"), sem("x2")
        s_st, s_mv, s_var, s_rs2, s_b2, s_hn, s_hg, s_h2 = (sem(x) for x in ("stats", "moments", "variance", "rstd2", "bias2", "hn", "h2_scaled", "h2"))
        s_ht, s_htk, s_lg, s_low, s_ex = sem("h2_turned"), sem("h2_t"), sem("logits"), sem("lowered"), sem("exp")
        s_sl = sem("slot_step")
        s_r, s_ch, s_bf, s_pl, s_id = sem("routing_step"), sem("chosen"), sem("before"), sem("places"), sem("index")
        s_x2o = [sem("x2_stored0"), sem("x2_stored1")]
        s_sc = [sem(f"scattered{i}") for i in range(4)]
        s_all, s_passed, s_passed_pool = sem("tables_stored"), sem("passed"), sem("passed_pool")
        block = mem.enter_context(nc.Block())

        def rows(name):
            return d[name].rearrange("(q t p) h -> q p t h", p=P, t=4)

        attn_q, x1_q, x2_q = rows("attn"), rows("x1"), rows("x2")

        def turns(eng, turn, lag):
            for n in range(4):
                turn(n, 0, n)
            with eng.Fori(1, Q // 4) as i:
                for n in range(4):
                    turn(4 * i + n, i, n)
            for n in range(lag):
                turn(Q + n, Q // 4, n)

        def early(q):
            return not (isinstance(q, int) and q >= Q)

        def late(q, lag):
            return not isinstance(q, int) or lag <= q < Q + lag

        def pairs(i, n, lag=0):
            return 2 * i + (n - lag) // 2

        @block.sync
        def _(sp):
            for to, frm in ((ident[:, :], d["ident"]), (tri[:, :], d["tri_ones"]), (ones[:, :], d["ones"]),
                            (lower[:, :, :].rearrange("p a b -> p (a b)"), d["lower"]), (slot_base[:, :], d["slot_base"]),
                            (mom[:, :, :], d["moments1"].rearrange("p (t k) -> p t k", k=2)),
                            (w_proj[:, :, :], d["L1_ffn_Wproj"].rearrange("(k p) h -> p k h", p=P)),
                            (w_gate[:, :, :], d["L1_ffn_Wgate"].rearrange("(k p) h -> p k h", p=P)),
                            (g_row[:, :], d["L1_ffn_ln2_g"].unsqueeze(0).to_broadcast([P, D])),
                            (b_row[:, :], d["L1_ffn_ln2_b"].unsqueeze(0).to_broadcast([P, D]))):
                sp.dma_start(to, frm).then_inc(s_in, 16)

            def load(q, n2):
                sp.dma_start(attn_in[n2][:, :, :], attn_q[q]).then_inc(s_a[n2], 16)
                sp.dma_start(x1_in[n2][:, :, :], x1_q[q]).then_inc(s_x1[n2], 16)

            load(0, 0)
            load(1, 1)

            def turn(q, i, n):
                if not (isinstance(q, int) and q + 2 >= Q):
                    sp.wait_ge(s_at, q + 1)
                    sp.wait_ge(s_xn, 4 * q + 4)
                    load(q + 2, n % 2)
                if early(q):
                    sp.wait_ge(s_x2, 2 * q + 2)
                    sp.dma_start(x2_q[q], x2[n % 2][:, :, :]).then_inc(s_x2o[n % 2], 16)

            for n in range(4):
                turn(n, 0, n)
            with sp.Fori(1, Q // 4 - 1) as i:
                for n in range(4):
                    turn(4 * i + n, i, n)
            for n in range(4):
                turn(Q - 4 + n, Q // 4 - 1, n)
            sp.wait_ge(s_id, 2 * Q)
            sp.dma_start(d["slots"], slots_all[:, :, :].rearrange("p q c -> p (q c)")).then_inc(s_all, 16)
            sp.dma_start(d["weights"], weights_all[:, :, :].rearrange("p q c -> p (q c)")).then_inc(s_all, 16)
            for n in range(2):
                sp.wait_ge(s_x2o[n], 16 * Q // 2)
            sp.wait_ge(s_all, 32)

        @block.gpsimd
        def _(pool):
            nc.gpsimd.memset(minus_half[:, :], -0.5).then_inc(s_half, 1)
            pool.wait_ge(s_half, 1)
            pool.wait_ge(s_pre, 1)
            nc.gpsimd.tensor_tensor(rstd1[:, :], small[:, :], minus_half[:, :], ALU.pow).then_inc(s_rs1, 1)

            def turn(q, i, n):
                if early(q):
                    pool.wait_ge(s_var, q + 1)
                    if not (isinstance(q, int) and q < 2):
                        pool.wait_ge(s_hn, q - 1)
                    nc.gpsimd.tensor_tensor(rstd2[n % 2][:, :], var[n % 2][:, :], minus_half[:, 0:4], ALU.pow).then_inc(s_rs2, 1)
                if late(q, 2):
                    wait_apart(pool, s_id, 2 * (q - 2) + 1, s_passed_pool)
                    for r in range(2):
                        for t in range(4):
                            m = (n - 2) % 4
                            pool.indirect_dma_start(d["expert_in"], bass.IndirectOffsetOnAxis(ap=idx[m][:, 4 * r + t:4 * r + t + 1], axis=0),
                                                    h2[m][:, t, :], None, bounds_check=E * CAP - 1, oob_is_err=False).then_inc(s_sc[m], 16)

            turns(pool, turn, 2)
            for m in range(4):
                pool.wait_ge(s_sc[m], 128 * Q // 4)

        @block.scalar
        def _(act):
            act.wait_ge(s_in, 160)
            act.wait_ge(s_pre, 2)

            def take_inputs(q, n2, loads):
                act.wait_ge(s_at, q + 1)
                need(act, s_pr, 2 * q - 2)
                for j in range(2):
                    ins = nc.scalar.activation(attn_t[n2][:, j, :], at_bank[j][:, :], ACT.Identity)
                ins.then_inc(s_atk, 1)
                act.wait_ge(s_x1[n2], loads)
                for t in range(4):
                    if t == 0:
                        need(act, s_x2, 2 * q - 2)
                    nc.scalar.activation(xn[n2][:, t, :], x1_in[n2][:, t, :], ACT.Identity, bias=bias1[:, bass.ds(4 * q + t, 1)],
                                         scale=rstd1[:, bass.ds(4 * q + t, 1)]).then_inc(s_xn, 1)

            def turn(q, i, n):
                n2 = n % 2
                if late(q, 1):
                    act.wait_ge(s_ht, q)
                    need(act, s_lg, q - 2)
                    for j in range(2):
                        ins = nc.scalar.activation(h2_t[1 - n2][:, j, :], ht_bank[j][:, :], ACT.Identity)
                    ins.then_inc(s_htk, 1)
                if not (isinstance(q, int) and q + 1 >= Q):
                    take_inputs(q + 1, 1 - n2, 16 * (2 * i + (n + 1) // 2) + 16)
                if late(q, 1):
                    act.wait_ge(s_low, q)
                    nc.scalar.activation(expd[:, :, :], lowered[:, :, :], ACT.Exp).then_inc(s_ex, 1)
                if early(q):
                    act.wait_ge(s_b2, q + 1)
                    need(act, s_h2, q - 1)
                    for t in range(4):
                        ins = nc.scalar.activation(hn[n2][:, t, :], x2[n2][:, t, :], ACT.Identity, bias=bias2[n2][:, t:t + 1], scale=rstd2[n2][:, t:t + 1])
                    ins.then_inc(s_hn, 1)

            take_inputs(0, 0, 16)
            for n in range(4):
                turn(n, 0, n)
            with act.Fori(1, Q // 4 - 1) as i:
                for n in range(4):
                    turn(4 * i + n, i, n)
            for n in range(5):
                turn(Q - 4 + n, Q // 4 - 1 + n // 4, n % 4)

        @block.vector
        def _(dve):
            dve.wait_ge(s_in, 160)
            nc.vector.memset(before[0][:, :], 0.0).then_inc(s_bf, 1)
            nc.vector.tensor_scalar(small[:, :], mom[:, :, 1], LN_EPS, None, ALU.add).then_inc(s_pre, 1)
            dve.wait_ge(s_rs1, 1)
            nc.vector.scalar_tensor_tensor(bias1[:, :], mom[:, :, 0], -1.0, rstd1[:, :], ALU.mult, ALU.mult).then_inc(s_pre, 1)

            def residual(q, i, n):
                n2 = n % 2
                for h in range(2):
                    dve.wait_ge(s_pr, 2 * q + h + 1)
                    dve.wait_ge(s_xn, 4 * q + 2 * h + 2)
                    if h == 0 and not (isinstance(q, int) and q < 2):
                        dve.wait_ge(s_x2o[n2], 16 * pairs(i, n))
                        dve.wait_ge(s_hn, q - 1)
                    nc.vector.tensor_tensor(x2[n2][:, 2 * h:2 * h + 2, :], pr_bank[h][:, :].rearrange("p (t c) -> p t c", t=2), xn[n2][:, 2 * h:2 * h + 2, :], ALU.add).then_inc(s_x2, 1)
                for t in range(4):
                    dve.wait_ge(s_x2, 2 * q + t // 2 + 1)
                    if t == 0:
                        need(dve, s_mv, 4 * q)
                    nc.vector.bn_stats(stats[:, t, :], x2[n2][:, t, :]).then_inc(s_st, 1)
                wait_apart(dve, s_st, 4 * q + 4, s_passed)
                for t in range(4):
                    nc.vector.bn_aggr(mv[n2][:, t, :], stats[:, t, :]).then_inc(s_mv, 1)
                dve.wait_ge(s_mv, 4 * q + 4)
                nc.vector.tensor_scalar(var[n2][:, :], mv[n2][:, :, 1], LN_EPS, None, ALU.add).then_inc(s_var, 1)

            def slots(q, i, n):
                n2 = n % 2
                e = SS * (q - 2)
                dve.wait_ge(s_pl, q - 1)
                place = place_bank[:, 0:4 * E].rearrange("p (t e) -> p t e", e=E)
                nc.vector.tensor_scalar(over[:, :, :], place, CAP + 0.5, None, ALU.is_gt).then_inc(s_sl, 1)
                nc.vector.tensor_tensor(slot[:, :, :], place, slot_base[:, :].unsqueeze(1).to_broadcast([P, 4, E]), ALU.add).then_inc(s_sl, 1)
                nc.vector.scalar_tensor_tensor(kept[:, :, :], place, CAP + 0.5, gates[n2][:, :, :], ALU.is_lt, ALU.mult).then_inc(s_sl, 1)
                for r in range(2):
                    nc.vector.tensor_scalar(sel[:, r, :], rank[n2][:, :, :].rearrange("p t e -> p (t e)"), float(r), None, ALU.is_equal).then_inc(s_sl, 1)
                dve.wait_ge(s_sl, e + 2)
                nc.vector.scalar_tensor_tensor(slot[:, :, :], over[:, :, :], float(E * CAP), slot[:, :, :], ALU.mult, ALU.add).then_inc(s_sl, 1)
                dve.wait_ge(s_sl, e + 5)
                nc.vector.tensor_tensor(picked_w[:, :, :], sel[:, :, :], kept[:, :, :].rearrange("p t e -> p (t e)").unsqueeze(1).to_broadcast([P, 2, 4 * E]), ALU.mult).then_inc(s_sl, 1)
                dve.wait_ge(s_sl, e + 6)
                nc.vector.tensor_tensor(picked[:, :, :], sel[:, :, :], slot[:, :, :].rearrange("p t e -> p (t e)").unsqueeze(1).to_broadcast([P, 2, 4 * E]), ALU.mult).then_inc(s_sl, 1)
                dve.wait_ge(s_sl, e + 8)
                nc.vector.tensor_reduce(slot_f[:, :], picked[:, :, :].rearrange("p r (t e) -> p (r t) e", e=E), AX_X, ALU.add).then_inc(s_sl, 1)
                nc.vector.tensor_reduce(weights_all[:, bass.ds(q - 2, 1), :], picked_w[:, :, :].rearrange("p r (t e) -> p (r t) e", e=E), AX_X, ALU.add).then_inc(s_sl, 1)
                dve.wait_ge(s_sl, e + 9)
                k = (n - 2) % 4
                if not (isinstance(q, int) and q < 6):
                    dve.wait_ge(s_sc[k], 128 * (i - 1 if n < 2 else i))
                nc.vector.tensor_copy(idx[k][:, :], slot_f[:, :]).then_inc(s_id, 1)
                nc.vector.tensor_scalar(slots_all[:, bass.ds(q - 2, 1), :].rearrange("p o c -> p (o c)"), slot_f[:, :], float(E * CAP - 1), None, ALU.min).then_inc(s_id, 1)

            def turn(q, i, n):
                n2 = n % 2
                m = 1 - n2
                if early(q):
                    residual(q, i, n)
                if late(q, 2):
                    slots(q, i, n)
                if late(q, 1):
                    e = RS * (q - 1)
                    dve.wait_ge(s_lg, q)
                    lg = lg_bank[:, 0:4 * E].rearrange("p (t e) -> p t e", e=E)
                    nc.vector.tensor_reduce(high[:, :], lg, AX_X, ALU.max).then_inc(s_r, 1)
                    dve.wait_ge(s_r, e + 1)
                    nc.vector.tensor_tensor(lowered[:, :, :], lg, high[:, :].unsqueeze(2).to_broadcast([P, 4, E]), ALU.subtract).then_inc(s_low, 1)
                if early(q):
                    dve.wait_ge(s_rs2, q + 1)
                    nc.vector.scalar_tensor_tensor(bias2[n2][:, :], mv[n2][:, :, 0], -1.0, rstd2[n2][:, :], ALU.mult, ALU.mult).then_inc(s_b2, 1)
                if late(q, 1):
                    dve.wait_ge(s_ex, q)
                    nc.vector.tensor_reduce(total[:, :], expd[:, :, :], AX_X, ALU.add).then_inc(s_r, 1)
                    dve.wait_ge(s_r, e + 2)
                    nc.vector.reciprocal(total[:, :], total[:, :]).then_inc(s_r, 1)
                    dve.wait_ge(s_r, e + 3)
                    nc.vector.tensor_tensor(gates[m][:, :, :], expd[:, :, :], total[:, :].unsqueeze(2).to_broadcast([P, 4, E]), ALU.mult).then_inc(s_r, 1)
                    dve.wait_ge(s_r, e + 4)
                    other = gates[m][:, :, :].unsqueeze(2).to_broadcast([P, 4, E, E])
                    own = gates[m][:, :, :].unsqueeze(3).to_broadcast([P, 4, E, E])
                    nc.vector.tensor_tensor(above[:, :, :, :], other, own, ALU.is_gt)
                    nc.vector.tensor_tensor(equal[:, :, :, :], other, own, ALU.is_equal).then_inc(s_r, 1)
                    dve.wait_ge(s_r, e + 5)
                    nc.vector.tensor_tensor(equal[:, :, :, :], equal[:, :, :, :], lower[:, :, :].unsqueeze(1).to_broadcast([P, 4, E, E]), ALU.mult).then_inc(s_r, 1)
                    dve.wait_ge(s_r, e + 6)
                    nc.vector.tensor_tensor(above[:, :, :, :], above[:, :, :, :], equal[:, :, :, :], ALU.add).then_inc(s_r, 1)
                    dve.wait_ge(s_r, e + 7)
                    nc.vector.tensor_reduce(rank[m][:, :, :], above[:, :, :, :], AX_X, ALU.add).then_inc(s_r, 1)
                    dve.wait_ge(s_r, e + 8)
                    nc.vector.tensor_scalar(chosen[m][:, :, :], rank[m][:, :, :], 1.5, None, ALU.is_lt).then_inc(s_ch, 1)
                    dve.wait_ge(s_ch, q)
                    nc.vector.tensor_reduce(chosen_sum[:, :], chosen[m][:, :, :].rearrange("p t e -> p e t"), AX_X, ALU.add).then_inc(s_r, 1)
                    dve.wait_ge(s_r, e + 9)
                    if not (isinstance(q, int) and q < 2):
                        dve.wait_ge(s_pl, q - 1)
                    nc.vector.tensor_tensor(before[1 - m][:, :], before[m][:, :], chosen_sum[:, :], ALU.add).then_inc(s_bf, 1)
                if early(q):
                    dve.wait_ge(s_hn, q + 1)
                    nc.vector.tensor_tensor(hn[n2][:, :, :], hn[n2][:, :, :], g_row[:, :].unsqueeze(1).to_broadcast([P, 4, D]), ALU.mult).then_inc(s_hg, 1)
                    dve.wait_ge(s_hg, q + 1)
                    if not (isinstance(q, int) and q < 4):
                        dve.wait_ge(s_sc[n], 128 * i)
                    nc.vector.tensor_tensor(h2[n][:, :, :], hn[n2][:, :, :], b_row[:, :].unsqueeze(1).to_broadcast([P, 4, D]), ALU.add).then_inc(s_h2, 1)

            turns(dve, turn, 2)

        @block.tensor
        def _(pe):
            pe.wait_ge(s_in, 160)

            def turn_attn(q, i, n):
                n2 = n % 2
                pe.wait_ge(s_a[n2], 16 * pairs(i, n) + 16)
                need(pe, s_atk, q)
                for j in range(2):
                    for t in range(4):
                        ins = nc.tensor.transpose(at_bank[j][:, t * P:(t + 1) * P], attn_in[n2][:, t, j * P:(j + 1) * P], ident[:, :])
                ins.then_inc(s_at, 1)

            def project(q, i, n):
                pe.wait_ge(s_atk, q + 1)
                for t in range(4):
                    if t % 2 == 0:
                        need(pe, s_x2, 2 * q + t // 2 - 1)
                    for j in range(2):
                        ins = nc.tensor.matmul(pr_bank[t // 2][:, (t % 2) * D:(t % 2 + 1) * D], attn_t[n % 2][:, j, t * P:(t + 1) * P], w_proj[:, j, :], start=(j == 0), stop=(j == 1))
                    if t % 2 == 1:
                        ins.then_inc(s_pr, 1)

            def turn_h2(q, n):
                pe.wait_ge(s_h2, q)
                if not (isinstance(q, int) and q == 1):
                    pe.wait_ge(s_htk, q - 1)
                for j in range(2):
                    for t in range(4):
                        ins = nc.tensor.transpose(ht_bank[j][:, t * P:(t + 1) * P], h2[(n - 1) % 4][:, t, j * P:(j + 1) * P], ident[:, :])
                ins.then_inc(s_ht, 1)

            def logits(q, n):
                pe.wait_ge(s_htk, q)
                if not (isinstance(q, int) and q == 1):
                    pe.wait_ge(s_low, q - 1)
                for t in range(4):
                    for j in range(2):
                        ins = nc.tensor.matmul(lg_bank[:, t * E:(t + 1) * E], h2_t[(n - 1) % 2][:, j, t * P:(t + 1) * P], w_gate[:, j, :], start=(j == 0), stop=(j == 1))
                ins.then_inc(s_lg, 1)

            def places(q, n):
                m = (n - 1) % 2
                pe.wait_ge(s_ch, q)
                pe.wait_ge(s_bf, q)
                if not (isinstance(q, int) and q == 1):
                    pe.wait_ge(s_id, 2 * (q - 1))
                mask = chosen[m]
                nc.tensor.matmul(place_bank[:, 0:4 * E], tri[:, :], mask[:, :, :], start=True, stop=False)
                for t in range(3):
                    later = 3 - t
                    nc.tensor.matmul(place_bank[:, (t + 1) * E:4 * E], ones[:, :], mask[:, t:t + 1, :].to_broadcast([P, later, E]), start=False, stop=False)
                nc.tensor.matmul(place_bank[:, 0:4 * E], ones[:, :], before[m][:, :].unsqueeze(1).to_broadcast([P, 4, E]), start=False, stop=True).then_inc(s_pl, 1)

            def turn(q, i, n):
                if early(q):
                    if isinstance(q, int) and q == 0:
                        turn_attn(0, 0, 0)
                    project(q, i, n)
                if late(q, 2):
                    places(q - 1, n - 1)
                if late(q, 1):
                    turn_h2(q, n)
                if not (isinstance(q, int) and q + 1 >= Q):
                    turn_attn(q + 1, i + (1 if n == 3 else 0), (n + 1) % 4)
                if late(q, 1):
                    logits(q, n)

            for n in range(4):
                turn(n, 0, n)
            with pe.Fori(1, Q // 4 - 1) as i:
                for n in range(4):
                    turn(4 * i + n, i, n)
            for n in range(6):
                turn(Q - 4 + n, Q // 4 - 1 + n // 4, n % 4)


def phase_combine(nc, ctx, d):
    Q = TILES // 4
    with ExitStack() as mem:
        def sb(name, shape, dt=F32):
            return mem.enter_context(nc.sbuf_tensor("cb_" + name, shape, dt))

        def sem(name):
            return ctx.enter_context(nc.semaphore("cb_" + name))

        slots_all = sb("slots_all", [P, TILES * 2], I32)
        weights_all = sb("weights_all", [P, TILES * 2])
        idx = [sb(f"idx{i}", [P, 8], I32) for i in range(2)]
        row = [sb(f"row{i}", [P, 8, D]) for i in range(2)]
        x1 = [sb(f"x1_{i}", [P, 4, D]) for i in range(2)]
        x2 = [sb(f"x2_{i}", [P, 4, D]) for i in range(2)]
        s1 = [sb(f"s1_{i}", [P, 4, D]) for i in range(2)]
        y1 = [sb(f"y1_{i}", [P, 4, D]) for i in range(2)]
        y = [sb(f"y_{i}", [P, 4, D]) for i in range(2)]
        gated = [sb(f"gated{i}", [P, 4, D]) for i in range(2)]
        prod = [sb(f"prod{i}", [P, 4, D]) for i in range(2)]
        res = [sb(f"res{i}", [P, 4, D]) for i in range(2)]

        s_in, s_id, s_passed = sem("in"), sem("index"), sem("passed")
        s_x1, s_x2, s_s1 = ([sem(f"{x}_loaded{i}") for i in range(2)] for x in ("x1", "x2", "s1"))
        s_row = [sem("rows0"), sem("rows1")]
        s_y1, s_y, s_g, s_p, s_res = sem("one_added"), sem("y"), sem("silu"), sem("product"), sem("result")
        s_out = [sem("stored0"), sem("stored1")]
        block = mem.enter_context(nc.Block())

        def rows(name):
            return d[name].rearrange("(q t p) h -> q p t h", p=P, t=4)

        def turns(eng, turn):
            for n in range(2):
                turn(n, 0, n)
            with eng.Fori(1, Q // 2 - 1) as i:
                for n in range(2):
                    turn(2 * i + n, i, n)
            for n in range(2):
                turn(Q - 2 + n, Q // 2 - 1, n)

        def before(q, n):
            return isinstance(q, int) and q < n

        @block.sync
        def _(sp):
            sp.dma_start(slots_all[:, :], d["slots"]).then_inc(s_in, 16)
            sp.dma_start(weights_all[:, :], d["weights"]).then_inc(s_in, 16)

            def load(q, n):
                sp.dma_start(x2[n][:, :, :], rows("x2")[q]).then_inc(s_x2[n], 16)
                sp.dma_start(s1[n][:, :, :], rows("s1")[q]).then_inc(s_s1[n], 16)
                sp.dma_start(x1[n][:, :, :], rows("x1")[q]).then_inc(s_x1[n], 16)

            load(0, 0)
            load(1, 1)

            def turn(q, i, n):
                sp.wait_ge(s_res, q + 1)
                sp.dma_start(rows("out")[q], res[n][:, :, :]).then_inc(s_out[n], 16)
                if not (isinstance(q, int) and q + 2 >= Q):
                    load(q + 2, n)

            turns(sp, turn)
            for n in range(2):
                sp.wait_ge(s_out[n], 16 * Q // 2)

        @block.gpsimd
        def _(pool):
            pool.wait_ge(s_in, 32)

            def gather(q, n):
                if not before(q, 2):
                    pool.wait_ge(s_y, 4 * q - 4)
                nc.gpsimd.tensor_copy(idx[n][:, :], slots_all[:, bass.ds(q * 8, 8)]).then_inc(s_id, 1)
                wait_apart(pool, s_id, q + 1, s_passed)
                for j in range(8):
                    pool.indirect_dma_start(row[n][:, j, :], None, d["expert_out"], bass.IndirectOffsetOnAxis(ap=idx[n][:, j:j + 1], axis=0),
                                            bounds_check=EXPERTS * CAP - 1, oob_is_err=False).then_inc(s_row[n], 16)

            turns(pool, lambda q, i, n: gather(q, n))

        @block.scalar
        def _(act):
            def turn(q, i, n):
                act.wait_ge(s_y, 4 * q + 4)
                if not before(q, 2):
                    act.wait_ge(s_p, q - 1)
                nc.scalar.activation(gated[n][:, :, :], y[n][:, :, :], ACT.Silu).then_inc(s_g, 1)

            turns(act, turn)

        @block.vector
        def _(dve):
            dve.wait_ge(s_in, 32)

            def finish(q, n):
                dve.wait_ge(s_g, q + 1)
                if not before(q, 2):
                    dve.wait_ge(s_res, q - 1)
                nc.vector.tensor_tensor(prod[n][:, :, :], gated[n][:, :, :], s1[n][:, :, :], ALU.mult).then_inc(s_p, 1)
                dve.wait_ge(s_p, q + 1)
                if not before(q, 2):
                    dve.wait_ge(s_out[n], 8 * q - 8 * n)
                nc.vector.tensor_tensor(res[n][:, :, :], prod[n][:, :, :], x1[n][:, :, :], ALU.add).then_inc(s_res, 1)

            def turn(q, i, n):
                dve.wait_ge(s_row[n], 128 * i + 128)
                dve.wait_ge(s_x2[n], 16 * i + 16)
                for t in range(4):
                    if t == 0 and not before(q, 2):
                        dve.wait_ge(s_y, 4 * q - 4)
                    nc.vector.scalar_tensor_tensor(y1[n][:, t, :], row[n][:, t, :], weights_all[:, bass.ds(8 * q + t, 1)], x2[n][:, t, :], ALU.mult, ALU.add).then_inc(s_y1, 1)
                for t in range(4):
                    dve.wait_ge(s_y1, 4 * q + t + 1)
                    if t == 0 and not before(q, 2):
                        dve.wait_ge(s_g, q - 1)
                    nc.vector.scalar_tensor_tensor(y[n][:, t, :], row[n][:, 4 + t, :], weights_all[:, bass.ds(8 * q + 4 + t, 1)], y1[n][:, t, :], ALU.mult, ALU.add).then_inc(s_y, 1)
                if not before(q, 1):
                    dve.wait_ge(s_s1[1 - n], 16 * i + 16 * n)
                    dve.wait_ge(s_x1[1 - n], 16 * i + 16 * n)
                    finish(q - 1, 1 - n)

            turns(dve, turn)
            dve.wait_ge(s_s1[1], 16 * Q // 2)
            dve.wait_ge(s_x1[1], 16 * Q // 2)
            finish(Q - 1, 1)


def build(nc, d):
    for phases in ((phase_l0, phase_ssm, phase_mlp, phase_qkv), (phase_attention, phase_gate, phase_moe, phase_combine)):
        with ExitStack() as ctx:
            first = ctx.enter_context(nc.semaphore(phases[0].__name__ + "_first"))
            for phase in phases:
                phase(nc, ctx, d)
            last = ctx.enter_context(nc.semaphore(phases[0].__name__ + "_last"))
        if phases[0] is phase_l0:
            nc.all_engine_barrier(sems_to_clear=range(first.num, last.num + 1))


def kernel(**inputs):
    import numpy as np
    import concourse.bacc as bacc
    from concourse.bass_utils import run_bass_kernel_spmd

    nc = bacc.Bacc("TRN2", target_bir_lowering=False, num_devices=1)
    d, arrays = {}, {}
    for name, a in {**inputs, **constants()}.items():
        a = np.ascontiguousarray(a)
        arrays["in_" + name] = a
        d[name] = nc.dram_tensor("in_" + name, a.shape, mybir.dt.from_np(a.dtype), kind="ExternalInput").ap()
    for name, (shape, dt) in SCRATCH.items():
        d[name] = nc.dram_tensor("scratch_" + name, shape, dt, kind="Internal").ap()
    out = nc.dram_tensor("out_0_dram", (B, L, D), F32, kind="ExternalOutput").ap()
    d["out"] = out.rearrange("b l h -> (b l) h")
    build(nc, d)
    r = run_bass_kernel_spmd(nc, [arrays], core_ids=[0])
    return r.results[0]["out_0_dram"]
```
